# Optimizing a Trainium2 kernel written in Bass

```python
import numpy as np
import jax
import jax.numpy as jnp

def _softmax(x, axis=-1):
    return jax.nn.softmax(x, axis=axis)

def _gelu(x):
    return jax.nn.gelu(x, approximate=True)

def _silu(x):
    return jax.nn.silu(x)

def _sigmoid(x):
    return jax.nn.sigmoid(x)

def _layernorm(x, axis=-1, eps=1e-05):
    m = jnp.mean(x, axis=axis, keepdims=True)
    v = jnp.var(x, axis=axis, keepdims=True)
    return (x - m) / jnp.sqrt(v + eps)

def _scatter_add(tgt, idx, src, axis=0):
    return tgt.at[idx].add(src)

def _segment_sum(src, seg, n):
    return jax.ops.segment_sum(src, seg, n)
kernel_name = 'mk_decoder_preln_d1_seqx_r4_db1b48'

def setup_inputs(seed: int=0):
    np.random.seed(seed)
    _w = jnp.asarray

    def _rec_inputs():
        import jax
        import jax.numpy as jnp
        _rk = jax.random.key(seed)
        x = 6.313e-05 + 0.9998 * jax.random.normal(jax.random.fold_in(_rk, 1), (4, 1024, 256), jnp.float32)
        _lenS = 1024 - jax.random.randint(jax.random.fold_in(_rk, 7), (4,), 0, max(1, 1024 // 4) + 1, jnp.int32)
        _lenS2 = 77 - jax.random.randint(jax.random.fold_in(_rk, 8), (4,), 0, max(1, 77 // 4) + 1, jnp.int32)
        _ctx_1024P = jax.random.normal(jax.random.fold_in(_rk, 11), (4, 16, 256), jnp.float32)
        _ctx_1024c = jax.random.dirichlet(jax.random.fold_in(_rk, 511), 0.3 * jnp.ones((16,), jnp.float32), (4, 77))
        _ctx_1024t = jnp.einsum('bsk,bkd->bsd', _ctx_1024c, _ctx_1024P)
        _ctx_1024t = _ctx_1024t * jax.lax.rsqrt(jnp.mean(jnp.square(_ctx_1024t)) + 1e-12) * 0.953939
        ctx_1024 = -0.000214406 + 1.00034 * (_ctx_1024t + 0.3 * jax.random.normal(jax.random.fold_in(_rk, 611), (4, 77, 256), jnp.float32))
        return (x, ctx_1024)
    x, ctx_1024 = _rec_inputs()

    def _L0_attn_setup():
        import jax, jax.numpy as jnp
        import numpy as np
        EPS = 1e-05
        NUM_HEADS = 16
        FEATURE_DIM = 16
        CHUNK = 64

        def _phi(x):
            f = x.shape[-1]
            return (x[..., :, None] * x[..., None, :]).reshape(*x.shape[:-1], f * f)
        key = jax.random.key(seed)
        ks = jax.random.split(key, 5)
        b, l, d = (4, 512, 256)
        h, f = (NUM_HEADS, FEATURE_DIM)
        hd = d // h
        scale = 0.02
        return {'hidden_states': jax.random.normal(ks[0], (b, l, d), jnp.float32), 'Wq': jax.random.normal(ks[1], (d, h * f), jnp.float32) * scale, 'Wk': jax.random.normal(ks[2], (d, h * f), jnp.float32) * scale, 'Wv': jax.random.normal(ks[3], (d, h * hd), jnp.float32) * scale, 'Wo': jax.random.normal(ks[4], (h * hd, d), jnp.float32) * scale}
    _L0_attn_all = _L0_attn_setup()
    _L0_attn_in = {k: v for k, v in _L0_attn_all.items() if k in ('Wq', 'Wk', 'Wv', 'Wo')}
    del _L0_attn_all

    def _L0_xattn_setup():
        import jax, jax.numpy as jnp
        import numpy as np
        from jax import lax
        BIG = jnp.float32(1e+30)

        def _pairwise_euclidean(a, b):
            aa = jnp.sum(a * a, axis=-1)[:, None]
            bb = jnp.sum(b * b, axis=-1)[None, :]
            ab = a @ b.T
            return jnp.sqrt(jnp.maximum(aa + bb - 2.0 * ab, 0.0))

        def _dtw_cost(D):
            row0 = jnp.cumsum(D[0])

            def row_step(prev_row, d_row):
                first = d_row[0] + prev_row[0]

                def col_step(left, inp):
                    d_ij, up, diag = inp
                    r = d_ij + jnp.minimum(jnp.minimum(up, left), diag)
                    return (r, r)
                _, rest = lax.scan(col_step, first, (d_row[1:], prev_row[1:], prev_row[:-1]))
                row = jnp.concatenate([first[None], rest])
                return (row, row)
            _, rows = lax.scan(row_step, row0, D[1:])
            return jnp.concatenate([row0[None], rows], axis=0)

        def _backtrack(R, T1, T2):
            L = T1 + T2 - 1

            def step(carry, _):
                i, j, done = carry
                valid = jnp.logical_not(done)
                cd = jnp.where((i > 0) & (j > 0), R[jnp.maximum(i - 1, 0), jnp.maximum(j - 1, 0)], BIG)
                cu = jnp.where(i > 0, R[jnp.maximum(i - 1, 0), j], BIG)
                cl = jnp.where(j > 0, R[i, jnp.maximum(j - 1, 0)], BIG)
                choice = jnp.argmin(jnp.stack([cd, cu, cl]))
                ni = jnp.where(choice <= 1, i - 1, i)
                nj = jnp.where((choice == 0) | (choice == 2), j - 1, j)
                at_origin = (i == 0) & (j == 0)
                ni = jnp.where(at_origin, 0, ni)
                nj = jnp.where(at_origin, 0, nj)
                return ((ni, nj, done | at_origin), (i, j, valid))
            init = (jnp.int32(T1 - 1), jnp.int32(T2 - 1), jnp.bool_(False))
            _, (i_idx, j_idx, valid) = lax.scan(step, init, None, length=L)
            return (i_idx, j_idx, valid)

        def _align_one(small, large):
            T_small, d = small.shape
            T_large = large.shape[0]
            D = _pairwise_euclidean(small, large)
            R = _dtw_cost(D)
            i_idx, j_idx, valid = _backtrack(R, T_small, T_large)
            contrib = small[i_idx] * valid[:, None].astype(small.dtype)
            expanded = jnp.zeros((T_large, d), dtype=small.dtype).at[j_idx].add(contrib)
            return expanded
        key = jax.random.key(seed)
        k1, k2 = jax.random.split(key)
        teacher = jax.random.normal(k1, (16, 100, 256), dtype=jnp.float32)
        student = jax.random.normal(k2, (16, 150, 256), dtype=jnp.float32)
        return {'teacher_features': teacher, 'student_features': student}
    _L0_xattn_all = _L0_xattn_setup()
    _L0_xattn_in = {k: v for k, v in _L0_xattn_all.items() if k in ()}
    del _L0_xattn_all

    def _L0_ffn_setup():
        import jax, jax.numpy as jnp
        import numpy as np
        D_MODEL = 256
        EXPANSION = 4
        D_HIDDEN = D_MODEL * EXPANSION
        NUM_STAGES = int(np.log2(D_HIDDEN))

        def butterfly(y, weights, dim):
            lead = y.shape[:-1]
            for stage in range(weights.shape[0]):
                s = 2 ** stage
                nb = dim // (2 * s)
                yr = y.reshape(*lead, nb, 2, s)
                a = yr[..., 0, :]
                b = yr[..., 1, :]
                w = weights[stage].reshape(nb, s, 2, 2)
                na = w[..., 0, 0] * a + w[..., 0, 1] * b
                nb2 = w[..., 1, 0] * a + w[..., 1, 1] * b
                y = jnp.stack([na, nb2], axis=-2).reshape(*lead, dim)
            return y
        key = jax.random.key(seed)
        ks = jax.random.split(key, 6)
        B, S = (4, 512)
        x = jax.random.normal(ks[0], (B, S, D_MODEL), jnp.float32)
        W_exp = jax.random.normal(ks[1], (D_MODEL, D_HIDDEN), jnp.float32) * 0.02
        b_exp = jnp.zeros((D_HIDDEN,), jnp.float32)
        up_weights = jax.random.normal(ks[2], (NUM_STAGES, D_HIDDEN // 2, 2, 2), jnp.float32) * 0.02
        up_bias = jnp.zeros((D_HIDDEN,), jnp.float32)
        down_weights = jax.random.normal(ks[3], (NUM_STAGES, D_HIDDEN // 2, 2, 2), jnp.float32) * 0.02
        W_con = jax.random.normal(ks[4], (D_HIDDEN, D_MODEL), jnp.float32) * 0.02
        b_con = jnp.zeros((D_MODEL,), jnp.float32)
        down_bias = jnp.zeros((D_MODEL,), jnp.float32)
        return dict(x=x, W_exp=W_exp, b_exp=b_exp, up_weights=up_weights, up_bias=up_bias, down_weights=down_weights, W_con=W_con, b_con=b_con, down_bias=down_bias)
    _L0_ffn_all = _L0_ffn_setup()
    _L0_ffn_in = {k: v for k, v in _L0_ffn_all.items() if k in ('W_exp', 'b_exp', 'up_weights', 'up_bias', 'down_weights', 'W_con', 'b_con', 'down_bias')}
    del _L0_ffn_all
    return {'x': x, 'ctx_1024': ctx_1024, 'L0_attn_Wq': _L0_attn_in['Wq'], 'L0_attn_Wk': _L0_attn_in['Wk'], 'L0_attn_Wv': _L0_attn_in['Wv'], 'L0_attn_Wo': _L0_attn_in['Wo'], 'L0_ffn_W_exp': _L0_ffn_in['W_exp'], 'L0_ffn_b_exp': _L0_ffn_in['b_exp'], 'L0_ffn_up_weights': _L0_ffn_in['up_weights'], 'L0_ffn_up_bias': _L0_ffn_in['up_bias'], 'L0_ffn_down_weights': _L0_ffn_in['down_weights'], 'L0_ffn_W_con': _L0_ffn_in['W_con'], 'L0_ffn_b_con': _L0_ffn_in['b_con'], 'L0_ffn_down_bias': _L0_ffn_in['down_bias']}

def reference(x, ctx_1024, L0_attn_Wq, L0_attn_Wk, L0_attn_Wv, L0_attn_Wo, L0_ffn_W_exp, L0_ffn_b_exp, L0_ffn_up_weights, L0_ffn_up_bias, L0_ffn_down_weights, L0_ffn_W_con, L0_ffn_b_con, L0_ffn_down_bias):
    import jax
    import jax.numpy as jnp

    def _L0_attn_ref(hidden_states, Wq, Wk, Wv, Wo):
        import jax, jax.numpy as jnp
        import numpy as np
        EPS = 1e-05
        NUM_HEADS = 16
        FEATURE_DIM = 16
        CHUNK = 64

        def _phi(x):
            f = x.shape[-1]
            return (x[..., :, None] * x[..., None, :]).reshape(*x.shape[:-1], f * f)
        b, l, d = hidden_states.shape
        h, f = (NUM_HEADS, FEATURE_DIM)
        hd = d // h
        q = (hidden_states @ Wq).reshape(b, l, h, f).transpose(0, 2, 1, 3)
        k = (hidden_states @ Wk).reshape(b, l, h, f).transpose(0, 2, 1, 3)
        v = (hidden_states @ Wv).reshape(b, l, h, hd).transpose(0, 2, 1, 3)
        q = q * f ** (-0.5)
        n = l // CHUNK
        qc = q.reshape(b, h, n, CHUNK, f)
        kc = k.reshape(b, h, n, CHUNK, f)
        vc = v.reshape(b, h, n, CHUNK, hd)
        phi_q = _phi(qc)
        phi_k = _phi(kc)
        mask = jnp.tril(jnp.ones((CHUNK, CHUNK), dtype=q.dtype))

        def step(carry, inp):
            S, z = carry
            pq, pk, qi, ki, vi = inp
            inter_o = jnp.einsum('bhcf,bhfd->bhcd', pq, S)
            inter_z = jnp.einsum('bhcf,bhf->bhc', pq, z)
            A = jnp.einsum('bhcf,bhsf->bhcs', qi, ki) ** 2 * mask
            intra_o = jnp.einsum('bhcs,bhsd->bhcd', A, vi)
            intra_z = A.sum(-1)
            o = (inter_o + intra_o) / (inter_z + intra_z + EPS)[..., None]
            S = S + jnp.einsum('bhcf,bhcd->bhfd', pk, vi)
            z = z + pk.sum(2)
            return ((S, z), o)
        f2 = f * f
        S0 = jnp.zeros((b, h, f2, hd), q.dtype)
        z0 = jnp.zeros((b, h, f2), q.dtype)
        xs = (jnp.moveaxis(phi_q, 2, 0), jnp.moveaxis(phi_k, 2, 0), jnp.moveaxis(qc, 2, 0), jnp.moveaxis(kc, 2, 0), jnp.moveaxis(vc, 2, 0))
        _, o = jax.lax.scan(step, (S0, z0), xs)
        o = jnp.moveaxis(o, 0, 2).reshape(b, h, l, hd)
        o = o.transpose(0, 2, 1, 3).reshape(b, l, h * hd)
        return o @ Wo

    def _L0_xattn_ref(teacher_features, student_features):
        import jax, jax.numpy as jnp
        import numpy as np
        from jax import lax
        BIG = jnp.float32(1e+30)

        def _pairwise_euclidean(a, b):
            aa = jnp.sum(a * a, axis=-1)[:, None]
            bb = jnp.sum(b * b, axis=-1)[None, :]
            ab = a @ b.T
            return jnp.sqrt(jnp.maximum(aa + bb - 2.0 * ab, 0.0))

        def _dtw_cost(D):
            row0 = jnp.cumsum(D[0])

            def row_step(prev_row, d_row):
                first = d_row[0] + prev_row[0]

                def col_step(left, inp):
                    d_ij, up, diag = inp
                    r = d_ij + jnp.minimum(jnp.minimum(up, left), diag)
                    return (r, r)
                _, rest = lax.scan(col_step, first, (d_row[1:], prev_row[1:], prev_row[:-1]))
                row = jnp.concatenate([first[None], rest])
                return (row, row)
            _, rows = lax.scan(row_step, row0, D[1:])
            return jnp.concatenate([row0[None], rows], axis=0)

        def _backtrack(R, T1, T2):
            L = T1 + T2 - 1

            def step(carry, _):
                i, j, done = carry
                valid = jnp.logical_not(done)
                cd = jnp.where((i > 0) & (j > 0), R[jnp.maximum(i - 1, 0), jnp.maximum(j - 1, 0)], BIG)
                cu = jnp.where(i > 0, R[jnp.maximum(i - 1, 0), j], BIG)
                cl = jnp.where(j > 0, R[i, jnp.maximum(j - 1, 0)], BIG)
                choice = jnp.argmin(jnp.stack([cd, cu, cl]))
                ni = jnp.where(choice <= 1, i - 1, i)
                nj = jnp.where((choice == 0) | (choice == 2), j - 1, j)
                at_origin = (i == 0) & (j == 0)
                ni = jnp.where(at_origin, 0, ni)
                nj = jnp.where(at_origin, 0, nj)
                return ((ni, nj, done | at_origin), (i, j, valid))
            init = (jnp.int32(T1 - 1), jnp.int32(T2 - 1), jnp.bool_(False))
            _, (i_idx, j_idx, valid) = lax.scan(step, init, None, length=L)
            return (i_idx, j_idx, valid)

        def _align_one(small, large):
            T_small, d = small.shape
            T_large = large.shape[0]
            D = _pairwise_euclidean(small, large)
            R = _dtw_cost(D)
            i_idx, j_idx, valid = _backtrack(R, T_small, T_large)
            contrib = small[i_idx] * valid[:, None].astype(small.dtype)
            expanded = jnp.zeros((T_large, d), dtype=small.dtype).at[j_idx].add(contrib)
            return expanded
        return jax.vmap(_align_one)(teacher_features, student_features)

    def _L0_ffn_ref(x, W_exp, b_exp, up_weights, up_bias, down_weights, W_con, b_con, down_bias):
        import jax, jax.numpy as jnp
        import numpy as np
        D_MODEL = 256
        EXPANSION = 4
        D_HIDDEN = D_MODEL * EXPANSION
        NUM_STAGES = int(np.log2(D_HIDDEN))

        def butterfly(y, weights, dim):
            lead = y.shape[:-1]
            for stage in range(weights.shape[0]):
                s = 2 ** stage
                nb = dim // (2 * s)
                yr = y.reshape(*lead, nb, 2, s)
                a = yr[..., 0, :]
                b = yr[..., 1, :]
                w = weights[stage].reshape(nb, s, 2, 2)
                na = w[..., 0, 0] * a + w[..., 0, 1] * b
                nb2 = w[..., 1, 0] * a + w[..., 1, 1] * b
                y = jnp.stack([na, nb2], axis=-2).reshape(*lead, dim)
            return y
        h = jnp.einsum('bsd,dh->bsh', x, W_exp) + b_exp
        h = butterfly(h, up_weights, D_HIDDEN)
        h = jax.nn.gelu(h + up_bias, approximate=False)
        h = butterfly(h, down_weights, D_HIDDEN)
        y = jnp.einsum('bsh,hd->bsd', h, W_con) + b_con
        return y + down_bias
    x = x + _L0_attn_ref(_layernorm(x, axis=-1), L0_attn_Wq, L0_attn_Wk, L0_attn_Wv, L0_attn_Wo)
    x = x + _L0_xattn_ref(ctx_1024, _layernorm(x, axis=-1))
    x = x + _L0_ffn_ref(_layernorm(x, axis=-1), L0_ffn_W_exp, L0_ffn_b_exp, L0_ffn_up_weights, L0_ffn_up_bias, L0_ffn_down_weights, L0_ffn_W_con, L0_ffn_b_con, L0_ffn_down_bias)
    return x

_drawn_inputs = setup_inputs


def setup_inputs(seed=0):
    import zlib

    import numpy as np

    out = dict(_drawn_inputs(seed))
    spreads = {'L0_ffn_b_exp': (0.0, 0.1),
     'L0_ffn_up_bias': (0.0, 0.1),
     'L0_ffn_b_con': (0.0, 0.1),
     'L0_ffn_down_bias': (0.0, 0.1)}
    factors = {'L0_attn_Wq': 7.132, 'L0_attn_Wk': 6.892, 'L0_attn_Wv': 5.319, 'L0_attn_Wo': 5.216}
    for name, (base, spread) in spreads.items():
        noise = np.random.default_rng([zlib.crc32(name.encode()), seed]).standard_normal(out[name].shape)
        drawn = base * np.exp(spread * noise) if base else spread * noise
        out[name] = jnp.asarray(drawn.astype(out[name].dtype))
    for name, factor in factors.items():
        out[name] = (out[name] * factor).astype(out[name].dtype)
    return out
```

```python
from contextlib import ExitStack

import concourse.bass as bass
from concourse import mybir

F32 = mybir.dt.float32
BF16 = mybir.dt.bfloat16
ALU = mybir.AluOpType
ACT = mybir.ActivationFunctionType
AX = mybir.AxisListType

P = 128
B, L, D = 4, 1024, 256
NH, HD = 16, 16
S = 77
HID = 1024
KD = D // P
TT = L // P
HALF = 512
HT = HID // P
NG = 4
GH = NH // NG
PARTS = 3
Q_PART = [0, 0, 0, 1, 1, 2]
K_PART = [0, 1, 2, 0, 1, 0]
STACK = len(Q_PART) * HD
LN_EPS, Z_EPS = 1e-5, 1e-5
W_BLK = 16
CB = L // W_BLK
T = S + W_BLK - 1
UNROLL = 4
BIG = 1e30
N_STAGE = 10
DC = D + 1


def attention_steps():
    return [(g, qc, kt) for g in range(NG) for qc in range(L // HALF) for kt in range((qc + 1) * HALF // P)]


def layer(nc, x, ctx_in, Wq, Wk, Wv, Wo, W_exp, b_exp, up_w, up_b, down_w, W_con, b_con, down_b, out):
    steps = attention_steps()
    NS = len(steps)
    diag = [n for n, (g, qc, kt) in enumerate(steps) if kt * P >= qc * HALF]
    last_of = [n for n, (g, qc, kt) in enumerate(steps) if (kt + 1) * P == (qc + 1) * HALF]
    NO = len(last_of)

    def span(n):
        g, qc, kt = steps[n]
        q0 = max(qc * HALF, kt * P)
        return q0, (qc + 1) * HALF - q0

    ITEMS = 2 * KD + 8 + TT // 2 + TT // 2 + 2 * KD + 2
    I_QK, I_V, I_WO, I_T2, I_D = 4, 12, 16, 20, 24
    SETUP_ITEMS = B + 4
    P1_BASE = SETUP_ITEMS
    P2_BASE = P1_BASE + B * ITEMS
    P2_ITEMS = 4 + B * TT // 2
    P3_BASE = P2_BASE + P2_ITEMS
    ITEMS3 = 4 + TT // 2
    assert ITEMS % 2 == 0 and SETUP_ITEMS % 2 == 0 and P2_ITEMS % 2 == 0 and ITEMS3 % 2 == 0

    qk_dram = nc.dram_tensor("qk_parts", (2, PARTS, D, L), BF16, kind="Internal").ap()
    dist_dram = nc.dram_tensor("dist", (B, S, L), F32, kind="Internal").ap()
    path_dram = nc.dram_tensor("path", (B, S, L), F32, kind="Internal").ap()
    mix_dram = nc.dram_tensor("mix", (HID, DC), F32, kind="Internal").ap()

    with ExitStack() as ctx:
        def sb(name, shape, dt=F32):
            return ctx.enter_context(nc.sbuf_tensor(name, shape, dt))

        def sem(name):
            return ctx.enter_context(nc.semaphore(name))

        X = sb("X", [P, B, TT, D])
        CTX = sb("CTX", [S, B, D])
        CTXT = sb("CTXT", [P, B, KD, S])
        AA = sb("AA", [S, B])
        IDENT = sb("IDENT", [P, P])
        ONES = sb("ONES", [P, S])
        MASK = sb("MASK", [P, P])
        WQKV = sb("WQKV", [P, KD, 3 * D])
        WOP = sb("WOP", [P, NG, D])
        BIAS = sb("BIAS", [P, D])
        BIAS2 = sb("BIAS2", [P, D])
        UPB = sb("UPB", [P, HT])
        BEFF = sb("BEFF", [P, HT])
        BEXP = sb("BEXP", [P, 8])
        SMALL = sb("SMALL", [P, 1])
        MIXA = sb("MIXA", [P, 8, DC])
        MIXT = sb("MIXT", [P, 4, DC])
        W1R = sb("W1R", [P, 8, DC])
        W2E = sb("W2E", [P, HT, DC])
        COEF = sb("COEF", [P, 2 * N_STAGE, 4, 4])
        STATS = sb("STATS", [P, TT, 6])
        MV = sb("MV", [P, TT, 2])
        VE = sb("VE", [P, TT])
        SD = sb("SD", [P, TT])
        RS = sb("RS", [P, TT])
        CORNER = sb("CORNER", [P, 1])
        START = sb("START", [P, 1])
        CUR = sb("CUR", [P, UNROLL, CB + 1])
        MIN2 = sb("MIN2", [P, CB])
        MARK = sb("MARK", [P, UNROLL, CB + 1])
        MOVE = sb("MOVE", [P, CB + 1])
        ENTER = sb("ENTER", [P, CB])
        XN = sb("XN", [P, TT, D])
        XNT = sb("XNT", [P, KD, L])

        ARENA = sb("ARENA", [P, ARENA_WORDS])
        at = [0]

        def view(words, dt=F32):
            a = ARENA[:, at[0]:at[0] + words]
            at[0] += words
            assert at[0] <= ARENA_WORDS, at[0]
            return a if dt == F32 else a.bitcast(dt)

        QP = view(2 * 2 * PARTS * L // 2, BF16).rearrange("p (m s c t) -> p m s c t", m=2, s=2, c=PARTS)
        at[0] = 0
        SNT = view(KD * L).rearrange("p (k t) -> p k t", k=KD)
        SQT = view(KD * L).rearrange("p (k t) -> p k t", k=KD)
        DSQ = view(L)
        DN = view(L)
        QST = view(2 * GH * L // 2, BF16).rearrange("p (u j t) -> p u j t", u=2, j=GH)
        KST = view(2 * GH * L // 2, BF16).rearrange("p (u j t) -> p u j t", u=2, j=GH)
        V1 = view(TT * NH * 32).rearrange("p (t h e) -> p t h e", t=TT, h=NH)
        A = view(2 * GH * HALF).rearrange("p (u j q) -> p u j q", u=2, j=GH)
        ONT = view(NG * L).rearrange("p (g t) -> p g t", g=NG)
        ZR = view(HALF)
        R1 = ZR
        CTB = view(KD * S).rearrange("p (k s) -> p k s", k=KD)
        WE = A
        at[0] = 0
        DSK = view(T * CB).rearrange("p (t c) -> p t c", t=T)
        RSK = view((T + 1) * (CB + 1)).rearrange("p (t c) -> p t c", t=T + 1)
        LEFT_BACK = view(T * (CB + 1)).rearrange("p (t c) -> p t c", t=T)
        LEFT = LEFT_BACK[:, ::-1, ::-1]
        CODE_BACK = view((T + 1) * (CB + 1)).rearrange("p (t c) -> p t c", t=T + 1)
        CODE = CODE_BACK[:, ::-1]
        M2 = DSK
        UPM = CODE[:, 0:T, 0:CB]
        PATH = DSK
        PT = RSK.rearrange("p t c -> p (t c)")[0:S, 0:B * L].rearrange("p (b t) -> p b t", b=B)
        at[0] = 0
        HGE = view(2 * HT * HALF).rearrange("p (u m t) -> p u m t", u=2, m=HT)
        OUTB = view(2 * 2 * D).rearrange("p (u t d) -> p u t d", u=2, t=2)
        XB = view(TT * D).rearrange("p (t d) -> p t d", t=TT)
        W1E = MIXA.rearrange("p r d -> p (r d)")[:, 0:KD * HID].rearrange("p (k h) -> p k h", k=KD)

        psS = ctx.enter_context(nc.psum_tensor("psS", [P, 2, 2, HALF], F32))
        psO = ctx.enter_context(nc.psum_tensor("psO", [P, 2, HALF], F32))
        psW = ctx.enter_context(nc.psum_tensor("psW", [P, 2, HALF], F32))

        s_const = sem("s_const")
        s_w_in = sem("s_w_in")
        s_wop0 = sem("s_wop0")
        s_ctx_in = sem("s_ctx_in")
        s_we_in = sem("s_we_in")
        s_x_in = sem("s_x_in")
        s_ready = sem("s_ready")
        s_free = sem("s_free")
        s_vec = sem("s_vec")
        s_var = sem("s_var")
        s_sd = sem("s_sd")
        s_xn = sem("s_xn")
        s_part1 = sem("s_part1")
        s_split = sem("s_split")
        s_parts_out = sem("s_parts_out")
        s_stack = [sem("s_stack_even"), sem("s_stack_odd")]
        s_qk = sem("s_qk")
        s_sq = sem("s_sq")
        s_mask = sem("s_mask")
        s_av = sem("s_av")
        s_ont = sem("s_ont")
        s_ctb = sem("s_ctb")
        s_sqt = sem("s_sqt")
        s_dn = sem("s_dn")
        s_dist_out = sem("s_dist_out")
        s_dsk0 = sem("s_dsk0")
        s_dsk_in = sem("s_dsk_in")
        s_min = sem("s_min")
        s_halo = sem("s_halo")
        s_row = sem("s_row")
        s_hist = sem("s_hist")
        s_move = sem("s_move")
        s_enter = sem("s_enter")
        s_halo2 = sem("s_halo2")
        s_mark = sem("s_mark")
        s_path_out = sem("s_path_out")
        s_pt_in = sem("s_pt_in")
        s_mix = sem("s_mix")
        s_mix_dma = sem("s_mix_dma")
        s_hid = sem("s_hid")
        s_gelu = sem("s_gelu")
        s_out = [sem("s_out_even"), sem("s_out_odd")]

        LAYOUT = {"A": (P, 1), "C": (16, 8), "D": (2, 64), "B": (1, P)}
        UP = [("A", [0, 1, 2]), ("C", [3, 4, 5]), ("D", [6, 7, 8]), ("B", [9])]
        DOWN = [(name, list(reversed(stages))) for name, stages in reversed(UP)]
        LOWBIT = {"A": 0, "C": 3, "D": 6, "B": 7}

        def pieces(name, dram, n):
            hi, lo = LAYOUT[name]
            if lo == 1:
                return [(0, P, dram.rearrange("(p r) c -> p r c", r=n))]
            v = dram.rearrange("(h r l) c -> h l r c", h=hi, r=n)
            return [(h * lo, lo, v[h]) for h in range(hi)]

        block = ctx.enter_context(nc.Block())

        @block.sync
        def _(sp):
            for i, w in enumerate((Wq, Wk, Wv)):
                sp.dma_start(WQKV[:, :, i * D:(i + 1) * D], w.rearrange("(k p) n -> p k n", p=P)).then_inc(s_w_in, 16)
            sp.dma_start(CTX[:], ctx_in.rearrange("b s d -> s b d")).then_inc(s_ctx_in, 16)
            sp.dma_start(WE.rearrange("p u j q -> p (u j q)")[:, 0:KD * HID].rearrange("p (k h) -> p k h", k=KD),
                         W_exp.rearrange("(k p) h -> p k h", p=P)).then_inc(s_we_in, 16)
            sp.wait_ge(s_wop0, 1)
            for j in range(GH):
                sp.dma_start(WOP[32 * j:32 * j + HD], Wo.rearrange("(g j d) n -> j d g n", g=NG, j=GH)[j]).then_inc(s_w_in, 16)
            sp.dma_start(BIAS[:], b_con.rearrange("(a n) -> a n", a=1).to_broadcast([P, D])).then_inc(s_out[0], 16)
            sp.dma_start(BIAS2[:], down_b.rearrange("(a n) -> a n", a=1).to_broadcast([P, D])).then_inc(s_out[1], 16)
            sp.dma_start(UPB[:], up_b.rearrange("(m p) -> p m", p=P), allow_slow_non_contiguous=True).then_inc(s_dist_out, 16)

            def stack_loads(g):
                for slot in range(len(Q_PART)):
                    rows = slice(slot * HD, (slot + 1) * HD)
                    for i, (dst, part) in enumerate(((QST, Q_PART), (KST, K_PART))):
                        src = qk_dram[i, part[slot]].rearrange("(g j d) t -> g d j t", g=NG, j=GH)[g]
                        sp.dma_start(dst[rows, g % 2], src).then_inc(s_stack[g % 2], 16)

            with sp.Fori(0, B) as b:
                for m in range(2):
                    for i in range(2):
                        sp.wait_ge(s_split, b * 8 + 4 * m + 2 * i + 2)
                        dst = qk_dram[i].rearrange("c (m p) t -> m p c t", m=2)[m]
                        sp.dma_start(dst, QP[:, m, i]).then_inc(s_parts_out, 16)
                    sp.wait_ge(s_parts_out, b * 64 + 32 * (m + 1))
                    for g in (2 * m, 2 * m + 1):
                        if g >= 2:
                            sp.wait_ge(s_qk, b * 2 * NS + (g - 1) * 2 * NS // NG)
                        stack_loads(g)
                sp.wait_ge(s_dn, b * 2 + 2)
                sp.dma_start(dist_dram[b], DN[0:S]).then_inc(s_dist_out, 16)

            sp.wait_ge(s_dsk0, 1)
            dist_v = dist_dram.rearrange("b i (w c) -> w b i c", w=W_BLK)
            for w in range(W_BLK):
                sp.dma_start(DSK[w:w + 97:32, w:w + S], dist_v[w]).then_inc(s_dsk_in, 16)

            sp.wait_ge(s_hist, UNROLL + 2 * T)
            path_v = path_dram.rearrange("b i (w c) -> w b i c", w=W_BLK)
            for w in range(W_BLK):
                sp.dma_start(path_v[w], PATH[w:w + 97:32, w:w + S]).then_inc(s_path_out, 16)
            sp.wait_ge(s_path_out, 16 * W_BLK)
            sp.dma_start(PT, path_dram.rearrange("b i t -> i b t")).then_inc(s_pt_in, 16)

            with sp.Fori(0, B) as b:
                for i in range(TT // 2):
                    sp.wait_ge(s_free, P3_BASE + b * ITEMS3 + 4 + i + 1)
                    sp.dma_start(out[b].rearrange("(t p) d -> p t d", p=P)[:, 2 * i:2 * i + 2], OUTB[:, i % 2]).then_inc(s_out[i % 2], 16)
            for i in range(2):
                sp.wait_ge(s_out[i], 16 + 16 * B * TT // 4)

        @block.gpsimd
        def _(pool):
            n_const = [0]

            def const(ins):
                ins.then_inc(s_const, 1)
                n_const[0] += 1

            const(pool.memset(IDENT[:], 0.0))
            const(pool.memset(MASK[:], 1.0))
            const(pool.memset(ONES[:], 1.0))
            const(pool.memset(START[:], 0.0))
            const(pool.memset(CORNER[:], BIG))
            pool.wait_ge(s_const, n_const[0])
            const(pool.affine_select(out=IDENT[:], in_=IDENT[:], compare_op=ALU.not_equal, fill=1.0, base=0,
                                     pattern=[[-1, P]], channel_multiplier=1))
            const(pool.affine_select(out=MASK[:], in_=MASK[:], compare_op=ALU.is_ge, fill=0.0, base=0,
                                     pattern=[[1, P]], channel_multiplier=-1))
            for b in range(B):
                for col, at_w, v in ((START, W_BLK - 1, 1.0), (CORNER, 0, 0.0)):
                    pool.wait_ge(s_const, n_const[0])
                    const(pool.affine_select(out=col[:], in_=col[:], compare_op=ALU.not_equal, fill=v,
                                             base=-32 * b - at_w, pattern=[[0, 1]], channel_multiplier=1))
            assert n_const[0] == N_CONST

            for b in range(B):
                pool.dma_start(X[:, b], x[b].rearrange("(t p) d -> p t d", p=P)).then_inc(s_x_in, 16)
                pool.wait_ge(s_x_in, 16 * (b + 1))

            n_mix, n_dma = [0], [0]

            def load(dst, src):
                pool.dma_start(dst, src).then_inc(s_mix_dma, 16)
                n_dma[0] += 16

            def loaded():
                pool.wait_ge(s_mix_dma, n_dma[0])

            def mixed():
                pool.wait_ge(s_mix, n_mix[0])

            def mix(ins):
                ins.then_inc(s_mix, 1)
                n_mix[0] += 1

            for u, (plan, w) in enumerate(((UP, up_w), (DOWN, down_w))):
                for name, stages in plan:
                    for st in stages:
                        for p0, n, src in pieces(name, w[st].rearrange("q o i -> q (o i)"), 4):
                            load(COEF[p0:p0 + n, u * N_STAGE + st], src)
            load(BEXP[:], b_exp.rearrange("(p r) -> p r", r=8))

            def butterfly(plan, which, dst, width):
                for k, (name, stages) in enumerate(plan):
                    if k:
                        mixed()
                        for p0, n, v in pieces(plan[k - 1][0], mix_dram[:, 0:width], 8):
                            load(v, dst[p0:p0 + n, :, 0:width])
                        loaded()
                        for p0, n, v in pieces(name, mix_dram[:, 0:width], 8):
                            load(MIXA[p0:p0 + n, :, 0:width], v)
                    loaded()
                    src, to = MIXA, dst
                    if len(stages) % 2 == 0:
                        raise AssertionError("a group has an odd number of stages")
                    for st in stages:
                        c_n = 1 << (st - LOWBIT[name])
                        def halves(t):
                            return t[:, :, 0:width].rearrange("p (a x c) d -> p x a c d", x=2, c=c_n)
                        cf = COEF[:, which * N_STAGE + st].rearrange("p (a c) k -> p k a c", c=c_n)
                        tmp = MIXT[:, :, 0:width].rearrange("p (a c) d -> p a c d", c=c_n)
                        old, new = halves(src), halves(to)
                        shape = [P, 4 // c_n, c_n, width]
                        for o in range(2):
                            own = cf[:, 3 * o].unsqueeze(3).to_broadcast(shape)
                            other = cf[:, (1 + o) if which == 0 else (2 - o)].unsqueeze(3).to_broadcast(shape)
                            mixed()
                            mix(pool.tensor_tensor(out=new[:, o], in0=old[:, o], in1=own, op=ALU.mult))
                            mix(pool.tensor_tensor(out=tmp, in0=old[:, 1 - o], in1=other, op=ALU.mult))
                            mixed()
                            mix(pool.tensor_tensor(out=new[:, o], in0=new[:, o], in1=tmp, op=ALU.add))
                        src, to = to, src

            pool.wait_ge(s_free, SETUP_ITEMS)
            loaded()
            mix(pool.tensor_copy(MIXA[:, :, D], BEXP[:]))
            butterfly(UP, 0, W1R, DC)
            mixed()
            load(MIXA[:, :, 0:D], W_con.rearrange("(r p) d -> p r d", p=P))
            butterfly(DOWN, 1, W2E, D)
            mixed()
            for p0, n, v in pieces("A", mix_dram[:, 0:D], 8):
                load(v, W2E[p0:p0 + n, :, 0:D])
            loaded()
            for p0, n, v in pieces("B", mix_dram[:, 0:D], 8):
                load(W2E[p0:p0 + n, :, 0:D], v)
            loaded()
            assert (n_mix[0], n_dma[0]) == (N_MIX, N_MIX_DMA), (n_mix, n_dma)

        @block.scalar
        def _(act):
            def roots(value):
                act.wait_ge(s_var, value)
                nc.scalar.activation(SD[:], VE[:], ACT.Sqrt).then_inc(s_sd, 1)

            with act.Fori(0, B) as b:
                roots(b * 2 + 1)
                act.wait_ge(s_dist_out, b * 16 + 16)
                for i in range(8):
                    m, s, h = i // 4, (i // 2) % 2, i % 2
                    item = I_QK + i
                    act.wait_ge(s_ready, P1_BASE + b * ITEMS + item + 1)
                    nc.scalar.activation(QP[:, m, s, 0, h * HALF:(h + 1) * HALF], psW[:, item % 2], ACT.Copy,
                                         scale=0.25 if s == 0 else 1.0).then_inc(s_part1, 1)
                for n in range(NS):
                    q0, N = span(n)
                    for a in range(2):
                        act.wait_ge(s_qk, b * 2 * NS + 2 * n + a + 1)
                        if n >= 2:
                            act.wait_ge(s_av, b * NS + n - 1)
                        nc.scalar.activation(A[:, n % 2, 2 * a:2 * a + 2, 0:N], psS[:, a, :, 0:N],
                                             ACT.Square).then_inc(s_sq, 1)
                roots(b * 2 + 2)
                for i in range(4):
                    k, h = i // 2, i % 2
                    act.wait_ge(s_free, P1_BASE + b * ITEMS + I_T2 + i + 1)
                    nc.scalar.activation(SQT[:, k, h * HALF:(h + 1) * HALF], SNT[:, k, h * HALF:(h + 1) * HALF],
                                         ACT.Square).then_inc(s_sqt, 1)
                for h in range(2):
                    act.wait_ge(s_free, P1_BASE + b * ITEMS + I_D + h + 1)
                    nc.scalar.activation(DN[0:S, h * HALF:(h + 1) * HALF], DSQ[0:S, h * HALF:(h + 1) * HALF],
                                         ACT.Sqrt).then_inc(s_dn, 1)

            act.wait_ge(s_row, 1)
            nc.scalar.activation(RSK[:, 0], CUR[:, 0], ACT.Copy).then_inc(s_hist, UNROLL)
            with act.Fori(0, T // UNROLL) as i:
                for u in range(UNROLL):
                    act.wait_ge(s_row, i * UNROLL + u + 2)
                    nc.scalar.activation(RSK[:, bass.ds(i * UNROLL + u + 1, 1)], CUR[:, (u + 1) % UNROLL].unsqueeze(1),
                                         ACT.Copy).then_inc(s_hist, 1)
            with act.Fori(0, T // UNROLL) as i:
                for u in range(UNROLL):
                    act.wait_ge(s_mark, i * UNROLL + u + 2)
                    nc.scalar.activation(PATH[:, bass.ds(T - 1 - u - i * UNROLL, 1)],
                                         MARK[:, (u + 1) % UNROLL, 0:CB].unsqueeze(1), ACT.Copy).then_inc(s_hist, 1)

            with act.Fori(0, B) as b:
                roots(2 * B + b + 1)
                for h in range(2):
                    for m in range(HT):
                        n = h * HT + m
                        if m == 0:
                            act.wait_ge(s_ready, P3_BASE + b * ITEMS3)
                        act.wait_ge(s_hid, b * 2 * HT + n + 1)
                        nc.scalar.activation(HGE[:, h, m], psS[:, (n % 4) // 2, n % 2], ACT.Gelu,
                                             bias=BEFF[:, m:m + 1]).then_inc(s_gelu, 1)

        @block.vector
        def _(dve):
            n_vec = [0]

            def vec(ins):
                ins.then_inc(s_vec, 1)
                n_vec[0] += 1

            def settle():
                nc.vector.memset(SMALL[:], 0.0)

            vec(nc.vector.memset(WOP[:], 0.0))
            nc.vector.memset(V1[:, :, :, HD:32], 1.0).then_inc(s_wop0, 1)
            dve.wait_ge(s_ctx_in, 16)
            sqc = ONT.rearrange("p g t -> p (g t)")[0:S, 0:B * D].rearrange("p (b d) -> p b d", b=B)
            vec(nc.vector.tensor_tensor(out=sqc, in0=CTX[:], in1=CTX[:], op=ALU.mult))
            dve.wait_ge(s_vec, n_vec[0])
            vec(nc.vector.tensor_reduce(AA[:], sqc, axis=AX.X, op=ALU.add))
            for b in range(B):
                dve.wait_ge(s_ready, b + 1)
                nc.vector.tensor_scalar(CTXT[:, b], psW[:, b % 2, 0:KD * S].rearrange("p (k s) -> p k s", k=KD), -2.0, None,
                                        ALU.mult).then_inc(s_free, 1)
            for i in range(4):
                dve.wait_ge(s_ready, B + i + 1)
                nc.vector.tensor_copy(MIXA[:, 2 * i:2 * i + 2, 0:D], psW[:, i % 2].rearrange("p (r d) -> p r d", r=2)
                                      ).then_inc(s_free, 1)
            dve.wait_ge(s_free, SETUP_ITEMS)
            dve.wait_ge(s_out[0], 16)
            dve.wait_ge(s_out[1], 16)
            vec(nc.vector.tensor_tensor(out=BIAS[:], in0=BIAS[:], in1=BIAS2[:], op=ALU.add))
            SETUP_VEC = n_vec[0]

            def layernorm(b, base, per, off, var_value, xn_wait=None):
                settle()
                for t in range(TT):
                    ins = nc.vector.bn_stats(STATS[:, t], X[:, b, t])
                ins.then_inc(s_vec, 1)
                dve.wait_ge(s_vec, b * per + (base + off + 1))
                settle()
                for t in range(TT):
                    ins = nc.vector.bn_aggr(MV[:, t], STATS[:, t])
                ins.then_inc(s_vec, 1)
                dve.wait_ge(s_vec, b * per + (base + off + 2))
                nc.vector.tensor_scalar(VE[:], MV[:, :, 1], LN_EPS, None, ALU.add).then_inc(s_var, 1)
                dve.wait_ge(s_sd, var_value)
                nc.vector.reciprocal(RS[:], SD[:]).then_inc(s_vec, 1)
                dve.wait_ge(s_vec, b * per + (base + off + 3))
                for t in range(TT):
                    ins = nc.vector.tensor_scalar(XN[:, t], X[:, b, t], MV[:, t, 0:1], RS[:, t:t + 1],
                                                  ALU.subtract, ALU.mult)
                ins.then_inc(s_xn, 1)

            def take(item_value):
                dve.wait_ge(s_ready, item_value)

            PER = 3 + 8 + NO * 3 + 3
            with dve.Fori(0, B) as b:
                base = P1_BASE
                dve.wait_ge(s_x_in, b * 16 + 16)
                layernorm(b, SETUP_VEC, PER, 0, b * 2 + 1)
                for i in range(4):
                    k, h = i // 2, i % 2
                    take(b * ITEMS + (base + i + 1))
                    nc.vector.tensor_copy(XNT[:, k, h * HALF:(h + 1) * HALF], psW[:, i % 2]).then_inc(s_free, 1)
                dve.wait_ge(s_dist_out, b * 16 + 16)
                for i in range(8):
                    m, s, h = i // 4, (i // 2) % 2, i % 2
                    item = I_QK + i
                    part = [QP[:, m, s, c, h * HALF:(h + 1) * HALF] for c in range(PARTS)]
                    dve.wait_ge(s_part1, b * 8 + i + 1)
                    nc.vector.scalar_tensor_tensor(out=R1, in0=psW[:, item % 2], scalar=0.25 if s == 0 else 1.0,
                                                   in1=part[0], op0=ALU.mult, op1=ALU.subtract).then_inc(s_free, 1)
                    dve.wait_ge(s_free, b * ITEMS + (base + item + 1))
                    nc.vector.tensor_copy(part[1], R1).then_inc(s_vec, 1)
                    dve.wait_ge(s_vec, b * PER + (SETUP_VEC + 3 + i + 1))
                    nc.vector.tensor_tensor(out=part[2], in0=R1, in1=part[1], op=ALU.subtract).then_inc(s_split, 1)
                    if i < 7:
                        dve.wait_ge(s_split, b * 8 + i + 1)
                for i in range(TT // 2):
                    item = I_V + i
                    take(b * ITEMS + (base + item + 1))
                    for j in range(2):
                        ins = nc.vector.tensor_copy(
                            V1[:, 2 * i + j, :, 0:HD],
                            psW[:, item % 2, j * D:(j + 1) * D].rearrange("p (h e) -> p h e", h=NH))
                    ins.then_inc(s_free, 1)
                nm = 0
                for n in range(NS):
                    g, qc, kt = steps[n]
                    if n in diag:
                        dve.wait_ge(s_sq, b * 2 * NS + 2 * n + 2)
                        blk = A[:, n % 2, :, 0:P]
                        nc.vector.tensor_tensor(out=blk, in0=blk, in1=MASK[:].unsqueeze(1).to_broadcast([P, GH, P]),
                                                op=ALU.mult).then_inc(s_mask, 1)
                    if n in last_of:
                        o = last_of.index(n)
                        off = SETUP_VEC + 11 + 3 * o
                        dve.wait_ge(s_av, b * NS + n + 1)
                        if o:
                            dve.wait_ge(s_ont, b * NO + o)
                        settle()
                        nc.vector.stream_shuffle(ZR, psO[:, o % 2], ZMASK).then_inc(s_vec, 1)
                        dve.wait_ge(s_vec, b * PER + (off + 1))
                        nc.vector.tensor_scalar(ZR, ZR, Z_EPS, None, ALU.add).then_inc(s_vec, 1)
                        dve.wait_ge(s_vec, b * PER + (off + 2))
                        nc.vector.reciprocal(ZR, ZR).then_inc(s_vec, 1)
                        dve.wait_ge(s_vec, b * PER + (off + 3))
                        nc.vector.tensor_tensor(out=ONT[:, g, qc * HALF:(qc + 1) * HALF], in0=psO[:, o % 2], in1=ZR,
                                                op=ALU.mult).then_inc(s_ont, 1)
                for i in range(TT // 2):
                    item = I_WO + i
                    take(b * ITEMS + (base + item + 1))
                    xs = X[:, b, 2 * i:2 * i + 2]
                    nc.vector.tensor_tensor(out=xs, in0=xs, in1=psW[:, item % 2].rearrange("p (t d) -> p t d", t=2),
                                            op=ALU.add).then_inc(s_free, 1)
                dve.wait_ge(s_free, b * ITEMS + (base + I_WO + TT // 2))
                layernorm(b, SETUP_VEC, PER, 11 + 3 * NO, b * 2 + 2)
                nc.vector.tensor_copy(CTB, CTXT[:, b]).then_inc(s_ctb, 1)
                dve.wait_ge(s_parts_out, b * 64 + 64)
                for i in range(4):
                    k, h = i // 2, i % 2
                    item = I_T2 + i
                    take(b * ITEMS + (base + item + 1))
                    nc.vector.tensor_copy(SNT[:, k, h * HALF:(h + 1) * HALF], psW[:, item % 2]).then_inc(s_free, 1)
                for h in range(2):
                    item = I_D + h
                    take(b * ITEMS + (base + item + 1))
                    nc.vector.tensor_scalar(DSQ[0:S, h * HALF:(h + 1) * HALF], psW[0:S, item % 2], AA[:, bass.ds(b, 1)], 0.0,
                                            ALU.add, ALU.max).then_inc(s_free, 1)
            n_vec[0] = SETUP_VEC + B * PER

            dve.wait_ge(s_dist_out, 16 + 16 * B)
            nc.vector.memset(DSK[:], 0.0).then_inc(s_dsk0, 1)
            vec(nc.vector.memset(CUR[:], BIG))
            vec(nc.vector.memset(MARK[:], 0.0))
            dve.wait_ge(s_vec, n_vec[0])
            nc.vector.tensor_scalar(MARK[:, 0, CB:CB + 1], MARK[:, 0, CB:CB + 1], START[:], None, ALU.add).then_inc(s_mark, 1)
            nc.vector.tensor_copy(CUR[:, 0, 0:1], CORNER[:]).then_inc(s_row, 1)
            for i in range(4):
                take(P2_BASE + i + 1)
                k, h = i // 2, i % 2
                nc.vector.tensor_copy(W1E[:, k, h * HALF:(h + 1) * HALF], psW[:, i % 2]).then_inc(s_free, 1)
            vec(nc.vector.tensor_tensor(out=BEFF[:], in0=UPB[:], in1=W1R[:, :, D], op=ALU.add))
            dve.wait_ge(s_dsk_in, 16 * W_BLK)
            dve.wait_ge(s_vec, n_vec[0])
            with dve.Fori(0, T // UNROLL) as i:
                for u in range(UNROLL):
                    src, dst = CUR[:, u], CUR[:, (u + 1) % UNROLL]
                    dve.wait_ge(s_hist, i * UNROLL + u + 1)
                    dve.wait_ge(s_row, i * UNROLL + u + 1)
                    nc.vector.tensor_tensor(out=MIN2[:], in0=src[:, 1:CB + 1], in1=src[:, 0:CB], op=ALU.min).then_inc(s_min, 1)
                    nc.vector.stream_shuffle(dst[:, 0:1], src[:, CB:CB + 1], FROM_LEFT).then_inc(s_halo, 1)
                    dve.wait_ge(s_min, i * UNROLL + u + 1)
                    dve.wait_ge(s_halo, i * UNROLL + u + 1)
                    nc.vector.tensor_tensor_scan(dst[:, 1:CB + 1], MIN2[:], DSK[:, bass.ds(i * UNROLL + u, 1)].rearrange("p a c -> p (a c)"),
                                                 dst[:, 0:1], ALU.min, ALU.add).then_inc(s_row, 1)
            dve.wait_ge(s_hist, UNROLL + T)
            up, dg = RSK[:, 0:T, 1:CB + 1], RSK[:, 0:T, 0:CB]
            vec(nc.vector.tensor_tensor(out=M2, in0=up, in1=dg, op=ALU.min))
            vec(nc.vector.tensor_tensor(out=UPM, in0=up, in1=dg, op=ALU.is_lt))
            vec(nc.vector.memset(CODE[:, T], 1.0))
            vec(nc.vector.memset(CODE[:, 0:T, CB], 0.0))
            vec(nc.vector.memset(LEFT[:, :, CB], 0.0))
            dve.wait_ge(s_vec, n_vec[0])
            vec(nc.vector.tensor_scalar(UPM, UPM, -2.0, 1.0, ALU.mult, ALU.add))
            dve.wait_ge(s_vec, n_vec[0])
            vec(nc.vector.tensor_tensor(out=LEFT[:, :, 0:CB], in0=M2, in1=RSK[:, 1:T + 1, 0:CB], op=ALU.is_gt))
            dve.wait_ge(s_vec, n_vec[0])
            vec(nc.vector.scalar_tensor_tensor(out=CODE[:, 0:T, 0:CB], in0=LEFT[:, :, 0:CB], scalar=0.0, in1=UPM,
                                               op0=ALU.is_equal, op1=ALU.mult))
            dve.wait_ge(s_vec, n_vec[0])
            vec(nc.vector.stream_shuffle(LEFT[:, 0:T - 1, CB], LEFT[:, 1:T, 0], FROM_RIGHT))
            vec(nc.vector.stream_shuffle(CODE[:, 0:T - 1, CB], CODE[:, 1:T, 0], FROM_RIGHT))
            dve.wait_ge(s_vec, n_vec[0])
            with dve.Fori(0, T // UNROLL) as i:
                for u in range(UNROLL):
                    src, dst = MARK[:, u], MARK[:, (u + 1) % UNROLL]
                    dve.wait_ge(s_hist, i * UNROLL + (T + u + 1))
                    dve.wait_ge(s_mark, i * UNROLL + u + 1)
                    nc.vector.tensor_tensor(out=MOVE[:], in0=src, in1=CODE_BACK[:, bass.ds(i * UNROLL + u, 1)].rearrange("p a c -> p (a c)"),
                                            op=ALU.mult).then_inc(s_move, 1)
                    nc.vector.stream_shuffle(dst[:, CB:CB + 1], src[:, 0:1], FROM_RIGHT).then_inc(s_halo2, 1)
                    dve.wait_ge(s_move, i * UNROLL + u + 1)
                    nc.vector.scalar_tensor_tensor(out=ENTER[:], in0=MOVE[:, 0:CB], scalar=-1.0, in1=MOVE[:, 1:CB + 1],
                                                   op0=ALU.is_equal, op1=ALU.max).then_inc(s_enter, 1)
                    dve.wait_ge(s_enter, i * UNROLL + u + 1)
                    dve.wait_ge(s_halo2, i * UNROLL + u + 1)
                    left = LEFT_BACK[:, bass.ds(i * UNROLL + u, 1)].rearrange("p a c -> p (a c)")[:, 0:CB]
                    nc.vector.tensor_tensor_scan(dst[:, 0:CB][:, ::-1], left, ENTER[:, ::-1],
                                                 dst[:, CB:CB + 1], ALU.mult, ALU.add).then_inc(s_mark, 1)
            for i in range(B * TT // 2):
                item = 4 + i
                take(P2_BASE + item + 1)
                xs = X[:, i // 4, 2 * (i % 4):2 * (i % 4) + 2]
                nc.vector.tensor_tensor(out=xs, in0=xs, in1=psW[:, item % 2].rearrange("p (t d) -> p t d", t=2),
                                        op=ALU.add).then_inc(s_free, 1)
            dve.wait_ge(s_free, P3_BASE)

            base3 = n_vec[0]
            PER3 = 3 + 1
            with dve.Fori(0, B) as b:
                layernorm(b, base3, PER3, 0, b + (2 * B + 1))
                nc.vector.tensor_tensor(out=XB, in0=X[:, b], in1=BIAS[:].unsqueeze(1).to_broadcast([P, TT, D]),
                                        op=ALU.add).then_inc(s_vec, 1)
                for i in range(4):
                    k, h = i // 2, i % 2
                    take(b * ITEMS3 + (P3_BASE + i + 1))
                    nc.vector.tensor_copy(XNT[:, k, h * HALF:(h + 1) * HALF], psW[:, i % 2]).then_inc(s_free, 1)
                dve.wait_ge(s_vec, b * PER3 + (base3 + 4))
                for i in range(TT // 2):
                    take(b * ITEMS3 + (P3_BASE + 4 + i + 1))
                    dve.wait_ge(s_out[i % 2], b * (16 * TT // 4) + 16 * (i // 2 + 1))
                    nc.vector.tensor_tensor(out=OUTB[:, i % 2], in0=XB[:, 2 * i:2 * i + 2],
                                            in1=psW[:, i % 2].rearrange("p (t d) -> p t d", t=2),
                                            op=ALU.add).then_inc(s_free, 1)

        @block.tensor
        def _(pe):
            pe.wait_ge(s_const, N_CONST)
            pe.wait_ge(s_ctx_in, 16)
            for b in range(B):
                if b >= 2:
                    pe.wait_ge(s_free, b - 1)
                for k in range(KD):
                    ins = nc.tensor.transpose(psW[:, b % 2, k * S:(k + 1) * S], CTX[:, b, k * P:(k + 1) * P], IDENT[0:S, 0:S])
                ins.then_inc(s_ready, 1)
            pe.wait_ge(s_we_in, 16)
            we = WE.rearrange("p u j q -> p (u j q)")[:, 0:KD * HID].rearrange("p (k c r) -> p k r c", k=KD, r=8)
            for i in range(4):
                pe.wait_ge(s_free, B + i - 1)
                for r in range(2):
                    for k in range(KD):
                        o = r * D + k * P
                        ins = nc.tensor.transpose(psW[:, i % 2, o:o + P], we[:, k, 2 * i + r], IDENT[:])
                ins.then_inc(s_ready, 1)
            pe.wait_ge(s_w_in, 16 * (3 + GH))

            def turn(k, h, src, u):
                for t in range(4):
                    ins = nc.tensor.transpose(psW[:, u, t * P:(t + 1) * P], src[:, 4 * h + t, k * P:(k + 1) * P], IDENT[:])
                ins.then_inc(s_ready, 1)

            with pe.Fori(0, B) as b:
                def bank(item):
                    pe.wait_ge(s_free, b * ITEMS + (P1_BASE + item - 1))
                    return item % 2

                pe.wait_ge(s_xn, b * 2 + 1)
                for i in range(4):
                    turn(i // 2, i % 2, XN, bank(i))
                pe.wait_ge(s_free, b * ITEMS + (P1_BASE + 4))
                for i in range(8):
                    m, s, h = i // 4, (i // 2) % 2, i % 2
                    u = bank(I_QK + i)
                    for k in range(KD):
                        ins = nc.tensor.matmul(psW[:, u], WQKV[:, k, s * D + m * P:s * D + (m + 1) * P],
                                               XNT[:, k, h * HALF:(h + 1) * HALF], start=k == 0, stop=k == KD - 1)
                    ins.then_inc(s_ready, 1)
                for i in range(TT // 2):
                    u = bank(I_V + i)
                    for j in range(2):
                        t = 2 * i + j
                        for k in range(KD):
                            ins = nc.tensor.matmul(psW[:, u, j * D:(j + 1) * D], XNT[:, k, t * P:(t + 1) * P],
                                                   WQKV[:, k, 2 * D:3 * D], start=k == 0, stop=k == KD - 1)
                    ins.then_inc(s_ready, 1)
                pe.wait_ge(s_free, b * ITEMS + (P1_BASE + I_WO))

                def scores(n):
                    g, qc, kt = steps[n]
                    q0, N = span(n)
                    if n % (NS // NG) == 0:
                        per = 16 * 2 * len(Q_PART)
                        pe.wait_ge(s_stack[g % 2], b * 2 * per + per * (g // 2 + 1))
                    for a in range(2):
                        if n:
                            pe.wait_ge(s_sq, b * 2 * NS + 2 * n + a - 1)
                        for j in range(2):
                            ins = nc.tensor.matmul(psS[:, a, j, 0:N], KST[0:STACK, g % 2, 2 * a + j, kt * P:(kt + 1) * P],
                                                   QST[0:STACK, g % 2, 2 * a + j, q0:q0 + N], start=True, stop=True)
                        ins.then_inc(s_qk, 1)

                def values(n):
                    g, qc, kt = steps[n]
                    q0, N = span(n)
                    o = 2 * g + qc
                    pe.wait_ge(s_sq, b * 2 * NS + 2 * n + 2)
                    if n in diag:
                        pe.wait_ge(s_mask, b * len(diag) + diag.index(n) + 1)
                    if kt == 0 and o >= 2:
                        pe.wait_ge(s_ont, b * NO + o - 1)
                    for j in range(GH):
                        ins = nc.tensor.matmul(psO[32 * j:32 * j + 32, o % 2, q0 - qc * HALF:q0 - qc * HALF + N],
                                               V1[:, kt, GH * g + j], A[:, n % 2, j, 0:N],
                                               start=kt == 0, stop=n in last_of)
                    ins.then_inc(s_av, 1)

                scores(0)
                for n in range(NS):
                    if n + 1 < NS:
                        scores(n + 1)
                    values(n)
                pe.wait_ge(s_ont, b * NO + NO)
                for i in range(TT // 2):
                    u = bank(I_WO + i)
                    for j in range(2):
                        t = 2 * i + j
                        for g in range(NG):
                            ins = nc.tensor.matmul(psW[:, u, j * D:(j + 1) * D], ONT[:, g, t * P:(t + 1) * P], WOP[:, g],
                                                   start=g == 0, stop=g == NG - 1)
                    ins.then_inc(s_ready, 1)
                pe.wait_ge(s_xn, b * 2 + 2)
                for i in range(4):
                    turn(i // 2, i % 2, XN, bank(I_T2 + i))
                pe.wait_ge(s_free, b * ITEMS + (P1_BASE + I_D))
                pe.wait_ge(s_ctb, b + 1)
                for h in range(2):
                    u = bank(I_D + h)
                    cols = slice(h * HALF, (h + 1) * HALF)
                    for k in range(KD):
                        nc.tensor.matmul(psW[0:S, u], CTB[:, k], SNT[:, k, cols], start=k == 0, stop=False)
                    if h == 0:
                        pe.wait_ge(s_sqt, b * 4 + 4)
                    for k in range(KD):
                        ins = nc.tensor.matmul(psW[0:S, u], ONES[:], SQT[:, k, cols], start=False, stop=k == KD - 1)
                    ins.then_inc(s_ready, 1)

            pe.wait_ge(s_mix, N_MIX)
            pe.wait_ge(s_mix_dma, N_MIX_DMA)
            for i in range(4):
                k, h = i // 2, i % 2
                pe.wait_ge(s_free, P2_BASE + i - 1)
                for r in range(4):
                    ins = nc.tensor.transpose(psW[:, i % 2, r * P:(r + 1) * P], W1R[:, 4 * h + r, k * P:(k + 1) * P], IDENT[:])
                ins.then_inc(s_ready, 1)
            pe.wait_ge(s_pt_in, 16)
            for i in range(B * TT // 2):
                pe.wait_ge(s_free, P2_BASE + 4 + i - 1)
                for j in range(2):
                    t = 2 * (i % 4) + j
                    ins = nc.tensor.matmul(psW[:, i % 2, j * D:(j + 1) * D], PT[:, i // 4, t * P:(t + 1) * P], CTX[:, i // 4],
                                           start=True, stop=True)
                ins.then_inc(s_ready, 1)

            with pe.Fori(0, B) as b:
                pe.wait_ge(s_xn, b + (2 * B + 1))
                for i in range(4):
                    pe.wait_ge(s_free, b * ITEMS3 + (P3_BASE + i - 1))
                    turn(i // 2, i % 2, XN, i % 2)
                pe.wait_ge(s_free, b * ITEMS3 + (P3_BASE + 4))
                for h in range(2):
                    for m in range(HT):
                        n = h * HT + m
                        if n >= 4:
                            pe.wait_ge(s_gelu, b * 2 * HT + n - 3)
                        for k in range(KD):
                            ins = nc.tensor.matmul(psS[:, (n % 4) // 2, n % 2], W1E[:, k, m * P:(m + 1) * P],
                                                   XNT[:, k, h * HALF:(h + 1) * HALF], start=k == 0, stop=k == KD - 1)
                        ins.then_inc(s_hid, 1)
                for i in range(TT // 2):
                    h = i // 2
                    pe.wait_ge(s_free, b * ITEMS3 + (P3_BASE + 4 + i - 1))
                    pe.wait_ge(s_gelu, b * 2 * HT + (h + 1) * HT)
                    for j in range(2):
                        c = (2 * (i % 2) + j) * P
                        for m in range(HT):
                            ins = nc.tensor.matmul(psW[:, i % 2, j * D:(j + 1) * D], HGE[:, h, m, c:c + P], W2E[:, m, 0:D],
                                                   start=m == 0, stop=m == HT - 1)
                    ins.then_inc(s_ready, 1)


N_CONST = 5 + 2 + 2 * B
ARENA_WORDS = 27300
N_MIX = 1 + 2 * N_STAGE * 6
N_MIX_DMA = 16 * (2 * (3 * 1 + 3 * 16 + 3 * 2 + 1) + 1 + 2 * ((1 + 16) + (16 + 2) + (2 + 1)) + 1 + 2)
ZMASK = [16 + i for i in range(16)] * 2
FROM_LEFT = [W_BLK] + list(range(W_BLK - 1)) + list(range(W_BLK, 32))
FROM_RIGHT = list(range(1, 32)) + [31]

_INS = ['x', 'ctx_1024', 'L0_attn_Wq', 'L0_attn_Wk', 'L0_attn_Wv', 'L0_attn_Wo', 'L0_ffn_W_exp', 'L0_ffn_b_exp',
        'L0_ffn_up_weights', 'L0_ffn_up_bias', 'L0_ffn_down_weights', 'L0_ffn_W_con', 'L0_ffn_b_con', 'L0_ffn_down_bias']


def kernel(**inputs):
    import numpy as np
    import concourse.bacc as bacc
    from concourse.bass_utils import run_bass_kernel_spmd

    nc = bacc.Bacc("TRN2", target_bir_lowering=False, num_devices=1)
    arrays, args = {}, []
    for name in _INS:
        a = np.ascontiguousarray(inputs[name])
        arrays[f"in_{name}"] = a
        args.append(nc.dram_tensor(f"in_{name}", a.shape, mybir.dt.from_np(a.dtype), kind="ExternalInput").ap())
    args.append(nc.dram_tensor("out_0", (B, L, D), F32, kind="ExternalOutput").ap())
    layer(nc, *args)
    r = run_bass_kernel_spmd(nc, [arrays], core_ids=[0])
    return r.results[0]["out_0"]
```

```python
from contextlib import ExitStack

import concourse.bass as bass
from concourse import mybir

F32 = mybir.dt.float32
BF16 = mybir.dt.bfloat16
ALU = mybir.AluOpType
ACT = mybir.ActivationFunctionType
AX = mybir.AxisListType

P = 128
B, L, D = 4, 1024, 256
NH, HD = 16, 16
S = 77
HID = 1024
KD = D // P
TT = L // P
HALF = 512
HT = HID // P
NG = 4
GH = NH // NG
PARTS = 3
Q_PART = [0, 0, 0, 1, 1, 2]
K_PART = [0, 1, 2, 0, 1, 0]
STACK = len(Q_PART) * HD
LN_EPS, Z_EPS = 1e-5, 1e-5
W_BLK = 16
CB = L // W_BLK
T = S + W_BLK - 1
BIG = 1e30
N_STAGE = 10
DC = D + 1


def attention_steps():
    return [(g, qc, kt) for g in range(NG) for qc in range(L // HALF) for kt in range((qc + 1) * HALF // P)]


def norm_units(kind, b):
    return ([("stats", kind, b, i) for i in range(4)] + [("variance", kind, b), ("rstd", kind, b)]
            + [("normal", kind, b, i) for i in range(4)])


def make_plan():
    ns = len(attention_steps())
    pace = 38
    front = lambda b: norm_units("x", b) + [("turn_x", b, i) for i in range(4)] + [("qk", b, i) for i in range(8)]
    back = lambda b: norm_units("student", b) + [("turn_s", b, i) for i in range(4)] + [("dist", b, i) for i in range(2)]
    values = lambda b: [("value", b, i) for i in range(TT // 2)]
    plan = [("context", b) for b in range(B)] + [("w_exp", i) for i in range(4)]
    plan += front(0) + values(0) + [("scores", 0, 0)]
    for b in range(B):
        fill = (back(b - 1) if b else []) + (front(b + 1) if b + 1 < B else [])
        done = 0
        for n in range(ns):
            if n + 1 < ns:
                plan.append(("scores", b, n + 1))
            plan.append(("products", b, n))
            upto = min(len(fill), max(0, (n - 1) * pace // (ns - 4)))
            plan += fill[done:upto]
            done = max(done, upto)
        assert done == len(fill)
        if b + 1 < B:
            plan += values(b + 1) + [("scores", b + 1, 0)]
        plan += [("wo", b, i) for i in range(TT // 2)]
    plan += back(B - 1)
    plan += [("w1", i) for i in range(4)] + [("warp",)]

    def ready(b):
        return ([("along", b, i) for i in range(TT // 2)] + norm_units("ffn", b)
                + [("turn_f", b, i) for i in range(4)])
    plan += ready(0)
    for b in range(B):
        plan += [("hidden", b, 0, m) for m in range(HT)]
        more = ready(b + 1) if b + 1 < B else []
        for m in range(HT):
            plan.append(("hidden", b, 1, m))
            plan += more[m * len(more) // HT:(m + 1) * len(more) // HT]
        plan += [("out", b, i) for i in range(TT // 2)]
    return plan


ITEM_KINDS = ("context", "w_exp", "turn_x", "qk", "value", "wo", "turn_s", "dist", "w1", "along", "turn_f", "out")


def layer(nc, x, ctx_in, Wq, Wk, Wv, Wo, W_exp, b_exp, up_w, up_b, down_w, W_con, b_con, down_b, out):
    steps = attention_steps()
    NS = len(steps)
    diag = [n for n, (g, qc, kt) in enumerate(steps) if kt * P >= qc * HALF]
    last_of = [n for n, (g, qc, kt) in enumerate(steps) if (kt + 1) * P == (qc + 1) * HALF]
    NO = len(last_of)

    def span(n):
        g, qc, kt = steps[n]
        q0 = max(qc * HALF, kt * P)
        return q0, (qc + 1) * HALF - q0

    plan = make_plan()
    item_of = {u: k for k, u in enumerate(u for u in plan if u[0] in ITEM_KINDS)}
    norm_of = {u[1:3]: k for k, u in enumerate(u for u in plan if u[0] == "variance")}

    def made(*unit):
        return item_of[unit] + 1

    def bank(*unit):
        return item_of[unit] % 2

    qk_dram = nc.dram_tensor("qk_parts", (B, 2, PARTS, D, L), BF16, kind="Internal").ap()
    dist_dram = nc.dram_tensor("dist", (B, S, L), F32, kind="Internal").ap()
    path_dram = nc.dram_tensor("path", (B, S, L), F32, kind="Internal").ap()
    mix_dram = nc.dram_tensor("mix", (HID, DC), F32, kind="Internal").ap()

    with ExitStack() as ctx:
        def sb(name, shape, dt=F32):
            return ctx.enter_context(nc.sbuf_tensor(name, shape, dt))

        def sem(name):
            return ctx.enter_context(nc.semaphore(name))

        X = sb("X", [P, B, TT, D])
        CTX = sb("CTX", [S, B, D])
        CTXT = sb("CTXT", [P, B, KD, S])
        AA = sb("AA", [S, B])
        IDENT = sb("IDENT", [P, P])
        ONES = sb("ONES", [P, S])
        MASK = sb("MASK", [P, P])
        WQKV = sb("WQKV", [P, KD, 3 * D])
        WOP = sb("WOP", [P, 2, D])
        BIAS = sb("BIAS", [P, D])
        BIAS2 = sb("BIAS2", [P, D])
        UPB = sb("UPB", [P, HT])
        BEFF = sb("BEFF", [P, HT])
        BEXP = sb("BEXP", [P, 8])
        ZT = sb("ZT", [P, HALF // 32])
        MIXA = sb("MIXA", [P, 8, DC])
        MIXT = sb("MIXT", [P, 4, DC])
        W1R = sb("W1R", [P, 8, DC])
        W2E = sb("W2E", [P, HT, DC])
        COEF = sb("COEF", [P, 2 * N_STAGE, 4, 4])
        STATS = sb("STATS", [P, TT, 6])
        MV = sb("MV", [P, TT, 2])
        VE = sb("VE", [P, TT])
        SD = sb("SD", [P, TT])
        RS = sb("RS", [P, TT])
        CORNER = sb("CORNER", [P, 1])
        START = sb("START", [P, 1])
        MIN2 = sb("MIN2", [P, CB])
        MOVE = sb("MOVE", [P, CB + 1])
        ENTER = sb("ENTER", [P, CB])
        XN = sb("XN", [P, TT, D])
        XNT = sb("XNT", [P, KD, L])

        ARENA = sb("ARENA", [P, ARENA_WORDS])
        at = [0]

        def view(words, dt=F32):
            a = ARENA[:, at[0]:at[0] + words]
            at[0] += words
            assert at[0] <= ARENA_WORDS, at[0]
            return a if dt == F32 else a.bitcast(dt)

        QP = view(2 * 2 * PARTS * L // 2, BF16).rearrange("p (m s c t) -> p m s c t", m=2, s=2, c=PARTS)
        at[0] = 0
        SNT = view(KD * L).rearrange("p (k t) -> p k t", k=KD)
        SQT = view(KD * L).rearrange("p (k t) -> p k t", k=KD)
        DSQ = view(L)
        DN = view(L)
        QST = view(2 * GH * L // 2, BF16).rearrange("p (u j t) -> p u j t", u=2, j=GH)
        KST = view(2 * GH * L // 2, BF16).rearrange("p (u j t) -> p u j t", u=2, j=GH)
        V1 = view(TT * NH * 32).rearrange("p (t h e) -> p t h e", t=TT, h=NH)
        A = view(2 * GH * HALF).rearrange("p (u j q) -> p u j q", u=2, j=GH)
        ONT = view(2 * L).rearrange("p (g t) -> p g t", g=2)
        TR = view(HALF).rearrange("p (t e) -> p t e", e=32)
        TB = view(2 * HALF).rearrange("p (q t e) -> p q t e", q=2, e=32)
        R1 = view(HALF)
        WE = A
        at[0] = 0
        DSK = view(T * CB).rearrange("p (t c) -> p t c", t=T)
        at[0] = 0
        PATH = view((T + 1) * (CB + 1)).rearrange("p (t c) -> p t c", t=T + 1)
        RSK = view((T + 1) * (CB + 1)).rearrange("p (t c) -> p t c", t=T + 1)
        LEFT_BACK = view(T * (CB + 1)).rearrange("p (t c) -> p t c", t=T)
        LEFT = LEFT_BACK[:, ::-1, ::-1]
        CODE_BACK = view((T + 1) * (CB + 1)).rearrange("p (t c) -> p t c", t=T + 1)
        CODE = CODE_BACK[:, ::-1]
        M2 = DSK
        UPM = CODE[:, 0:T, 0:CB]
        at[0] = 0
        HGE = view(2 * HT * HALF).rearrange("p (u m t) -> p u m t", u=2, m=HT)
        OUTB = view(2 * 2 * D).rearrange("p (u t d) -> p u t d", u=2, t=2)
        XFT = [XNT, view(KD * L).rearrange("p (k t) -> p k t", k=KD)]
        XB = view(TT * D).rearrange("p (t d) -> p t d", t=TT)
        PT = view(B * L)[0:S].rearrange("p (b t) -> p b t", b=B)
        W1E = MIXA.rearrange("p r d -> p (r d)")[:, 0:KD * HID].rearrange("p (k h) -> p k h", k=KD)

        psS = ctx.enter_context(nc.psum_tensor("psS", [P, 2, 2, HALF], F32))
        psO = ctx.enter_context(nc.psum_tensor("psO", [P, 2, HALF], F32))
        psW = ctx.enter_context(nc.psum_tensor("psW", [P, 2, HALF], F32))

        s_const = sem("s_const")
        s_w_in = sem("s_w_in")
        s_ones = sem("s_ones")
        s_ctx_in = sem("s_ctx_in")
        s_we_in = sem("s_we_in")
        s_bias_in = sem("s_bias_in")
        s_x_in = sem("s_x_in")
        s_ready = sem("s_ready")
        s_free = sem("s_free")
        s_vec = sem("s_vec")
        s_var = sem("s_var")
        s_sd = sem("s_sd")
        s_xn = sem("s_xn")
        s_part1 = sem("s_part1")
        s_split = sem("s_split")
        s_parts_out = sem("s_parts_out")
        s_stack = [sem("s_stack_even"), sem("s_stack_odd")]
        s_qk = sem("s_qk")
        s_sq = sem("s_sq")
        s_mask = sem("s_mask")
        s_av = sem("s_av")
        s_o_read = sem("s_o_read")
        s_ont = sem("s_ont")
        s_sqt = sem("s_sqt")
        s_dn = sem("s_dn")
        s_dist_out = sem("s_dist_out")
        s_dsk0 = sem("s_dsk0")
        s_dsk_in = sem("s_dsk_in")
        s_pre = sem("s_pre")
        s_row = sem("s_row")
        s_move = sem("s_move")
        s_enter = sem("s_enter")
        s_mark = sem("s_mark")
        s_path_out = sem("s_path_out")
        s_pt_in = sem("s_pt_in")
        s_mix = sem("s_mix")
        s_mix_dma = sem("s_mix_dma")
        s_hid = sem("s_hid")
        s_gelu = sem("s_gelu")
        s_out = [sem("s_out_even"), sem("s_out_odd")]

        LAYOUT = {"A": (P, 1), "C": (16, 8), "D": (2, 64), "B": (1, P)}
        UP = [("A", [0, 1, 2]), ("C", [3, 4, 5]), ("D", [6, 7, 8]), ("B", [9])]
        DOWN = [(name, list(reversed(stages))) for name, stages in reversed(UP)]
        LOWBIT = {"A": 0, "C": 3, "D": 6, "B": 7}

        def pieces(name, dram, n):
            hi, lo = LAYOUT[name]
            if lo == 1:
                return [(0, P, dram.rearrange("(p r) c -> p r c", r=n))]
            v = dram.rearrange("(h r l) c -> h l r c", h=hi, r=n)
            return [(h * lo, lo, v[h]) for h in range(hi)]

        block = ctx.enter_context(nc.Block())

        @block.sync
        def _(sp):
            for i, w in enumerate((Wq, Wk, Wv)):
                sp.dma_start(WQKV[:, :, i * D:(i + 1) * D], w.rearrange("(k p) n -> p k n", p=P)).then_inc(s_w_in, 16)
            sp.dma_start(CTX[:], ctx_in.rearrange("b s d -> s b d")).then_inc(s_ctx_in, 16)
            sp.dma_start(WE.rearrange("p u j q -> p (u j q)")[:, 0:KD * HID].rearrange("p (k h) -> p k h", k=KD),
                         W_exp.rearrange("(k p) h -> p k h", p=P)).then_inc(s_we_in, 16)
            for j in range(GH):
                for e in range(2):
                    sp.dma_start(WOP[32 * j + HD * e:32 * j + HD * (e + 1)],
                                 Wo.rearrange("(g e j d) n -> j e d g n", g=2, e=2, j=GH)[j, e]).then_inc(s_w_in, 16)
            sp.dma_start(BIAS[:], b_con.rearrange("(a n) -> a n", a=1).to_broadcast([P, D])).then_inc(s_bias_in, 16)
            sp.dma_start(BIAS2[:], down_b.rearrange("(a n) -> a n", a=1).to_broadcast([P, D])).then_inc(s_bias_in, 16)
            sp.dma_start(UPB[:], up_b.rearrange("(m p) -> p m", p=P), allow_slow_non_contiguous=True).then_inc(s_bias_in, 16)

            def parts_out(b, m):
                for i in range(2):
                    sp.wait_ge(s_split, b * 8 + 4 * m + 2 * i + 2)
                    dst = qk_dram[b, i].rearrange("c (m p) t -> m p c t", m=2)[m]
                    sp.dma_start(dst, QP[:, m, i]).then_inc(s_parts_out, 16)
                sp.wait_ge(s_parts_out, b * 64 + 32 * (m + 1))

            def stack_in(b, g):
                if b * NG + g >= 2:
                    sp.wait_ge(s_qk, (b * NG + g - 1) * 2 * NS // NG)
                for slot in range(len(Q_PART)):
                    rows = slice(slot * HD, (slot + 1) * HD)
                    for i, (dst, part) in enumerate(((QST, Q_PART), (KST, K_PART))):
                        src = qk_dram[b, i, part[slot]].rearrange("(g j d) t -> g d j t", g=NG, j=GH)[g]
                        sp.dma_start(dst[rows, g % 2], src).then_inc(s_stack[g % 2], 16)

            def dist_out(b):
                sp.wait_ge(s_dn, b * 2 + 2)
                sp.dma_start(dist_dram[b], DN[0:S]).then_inc(s_dist_out, 16)

            parts_out(0, 0)
            stack_in(0, 0)
            stack_in(0, 1)
            parts_out(0, 1)
            for b in range(B):
                stack_in(b, 2)
                if b:
                    dist_out(b - 1)
                stack_in(b, 3)
                if b + 1 < B:
                    for m in range(2):
                        parts_out(b + 1, m)
                        stack_in(b + 1, m)
            dist_out(B - 1)

            sp.wait_ge(s_dsk0, 1)
            sp.wait_ge(s_dist_out, 16 * B)
            dist_v = dist_dram.rearrange("b i (w c) -> w b i c", w=W_BLK)
            for w in range(W_BLK):
                sp.dma_start(DSK[w:w + 97:32, w:w + S], dist_v[w]).then_inc(s_dsk_in, 16)

            sp.wait_ge(s_mark, T + 1)
            path_v = path_dram.rearrange("b i (w c) -> w b i c", w=W_BLK)
            for w in range(W_BLK):
                sp.dma_start(path_v[w], PATH[w:w + 97:32, w:w + S, 0:CB]).then_inc(s_path_out, 16)
            sp.wait_ge(s_path_out, 16 * W_BLK)
            sp.dma_start(PT, path_dram.rearrange("b i t -> i b t")).then_inc(s_pt_in, 16)

            for b in range(B):
                for i in range(TT // 2):
                    sp.wait_ge(s_free, made("out", b, i))
                    sp.dma_start(out[b].rearrange("(t p) d -> p t d", p=P)[:, 2 * i:2 * i + 2], OUTB[:, i % 2]).then_inc(s_out[i % 2], 16)
            for i in range(2):
                sp.wait_ge(s_out[i], 16 * B * TT // 4)

        @block.gpsimd
        def _(pool):
            n_const = [0]

            def const(ins):
                ins.then_inc(s_const, 1)
                n_const[0] += 1

            const(pool.memset(IDENT[:], 0.0))
            const(pool.memset(MASK[:], 1.0))
            const(pool.memset(ONES[:], 1.0))
            const(pool.memset(START[:], 0.0))
            const(pool.memset(CORNER[:], BIG))
            pool.wait_ge(s_const, n_const[0])
            const(pool.affine_select(out=IDENT[:], in_=IDENT[:], compare_op=ALU.not_equal, fill=1.0, base=0,
                                     pattern=[[-1, P]], channel_multiplier=1))
            const(pool.affine_select(out=MASK[:], in_=MASK[:], compare_op=ALU.is_ge, fill=0.0, base=0,
                                     pattern=[[1, P]], channel_multiplier=-1))
            for b in range(B):
                for col, at_w, v in ((START, W_BLK - 1, 1.0), (CORNER, 0, 0.0)):
                    pool.wait_ge(s_const, n_const[0])
                    const(pool.affine_select(out=col[:], in_=col[:], compare_op=ALU.not_equal, fill=v,
                                             base=-32 * b - at_w, pattern=[[0, 1]], channel_multiplier=1))
            assert n_const[0] == N_CONST

            for b in range(B):
                pool.dma_start(X[:, b], x[b].rearrange("(t p) d -> p t d", p=P)).then_inc(s_x_in, 16)
                pool.wait_ge(s_x_in, 16 * (b + 1))

            n_mix, n_dma = [0], [0]

            def load(dst, src):
                pool.dma_start(dst, src).then_inc(s_mix_dma, 16)
                n_dma[0] += 16

            def loaded():
                pool.wait_ge(s_mix_dma, n_dma[0])

            def mixed():
                pool.wait_ge(s_mix, n_mix[0])

            def mix(ins):
                ins.then_inc(s_mix, 1)
                n_mix[0] += 1

            for u, (plan, w) in enumerate(((UP, up_w), (DOWN, down_w))):
                for name, stages in plan:
                    for st in stages:
                        for p0, n, src in pieces(name, w[st].rearrange("q o i -> q (o i)"), 4):
                            load(COEF[p0:p0 + n, u * N_STAGE + st], src)
            load(BEXP[:], b_exp.rearrange("(p r) -> p r", r=8))

            def butterfly(plan, which, dst, width):
                for k, (name, stages) in enumerate(plan):
                    if k:
                        mixed()
                        for p0, n, v in pieces(plan[k - 1][0], mix_dram[:, 0:width], 8):
                            load(v, dst[p0:p0 + n, :, 0:width])
                        loaded()
                        for p0, n, v in pieces(name, mix_dram[:, 0:width], 8):
                            load(MIXA[p0:p0 + n, :, 0:width], v)
                    loaded()
                    src, to = MIXA, dst
                    if len(stages) % 2 == 0:
                        raise AssertionError("a group has an odd number of stages")
                    for st in stages:
                        c_n = 1 << (st - LOWBIT[name])
                        def halves(t):
                            return t[:, :, 0:width].rearrange("p (a x c) d -> p x a c d", x=2, c=c_n)
                        cf = COEF[:, which * N_STAGE + st].rearrange("p (a c) k -> p k a c", c=c_n)
                        tmp = MIXT[:, :, 0:width].rearrange("p (a c) d -> p a c d", c=c_n)
                        old, new = halves(src), halves(to)
                        shape = [P, 4 // c_n, c_n, width]
                        for o in range(2):
                            own = cf[:, 3 * o].unsqueeze(3).to_broadcast(shape)
                            other = cf[:, (1 + o) if which == 0 else (2 - o)].unsqueeze(3).to_broadcast(shape)
                            mixed()
                            mix(pool.tensor_tensor(out=new[:, o], in0=old[:, o], in1=own, op=ALU.mult))
                            mix(pool.tensor_tensor(out=tmp, in0=old[:, 1 - o], in1=other, op=ALU.mult))
                            mixed()
                            mix(pool.tensor_tensor(out=new[:, o], in0=new[:, o], in1=tmp, op=ALU.add))
                        src, to = to, src

            pool.wait_ge(s_free, made("w_exp", 3))
            loaded()
            mix(pool.tensor_copy(MIXA[:, :, D], BEXP[:]))
            butterfly(UP, 0, W1R, DC)
            mixed()
            load(MIXA[:, :, 0:D], W_con.rearrange("(r p) d -> p r d", p=P))
            butterfly(DOWN, 1, W2E, D)
            mixed()
            for p0, n, v in pieces("A", mix_dram[:, 0:D], 8):
                load(v, W2E[p0:p0 + n, :, 0:D])
            loaded()
            for p0, n, v in pieces("B", mix_dram[:, 0:D], 8):
                load(W2E[p0:p0 + n, :, 0:D], v)
            loaded()
            assert (n_mix[0], n_dma[0]) == (N_MIX, N_MIX_DMA), (n_mix, n_dma)

        @block.scalar
        def _(act):
            for u in plan:
                kind = u[0]
                if kind == "variance":
                    act.wait_ge(s_var, norm_of[u[1:]] + 1)
                    nc.scalar.activation(SD[:], VE[:], ACT.Sqrt).then_inc(s_sd, 1)
                elif kind == "qk":
                    _, b, i = u
                    m, s, h = i // 4, (i // 2) % 2, i % 2
                    if i == 0 and b >= 2:
                        act.wait_ge(s_dist_out, 16 * (b - 1))
                    act.wait_ge(s_ready, made(*u))
                    nc.scalar.activation(QP[:, m, s, 0, h * HALF:(h + 1) * HALF], psW[:, bank(*u)], ACT.Copy,
                                         scale=0.25 if s == 0 else 1.0).then_inc(s_part1, 1)
                elif kind == "scores":
                    _, b, n = u
                    q0, N = span(n)
                    G = b * NS + n
                    for a in range(2):
                        act.wait_ge(s_qk, 2 * G + a + 1)
                        if G >= 2 and a == 0:
                            act.wait_ge(s_av, G - 1)
                        nc.scalar.activation(A[:, G % 2, 2 * a:2 * a + 2, 0:N], psS[:, a, :, 0:N],
                                             ACT.Square).then_inc(s_sq, 1)
                elif kind == "turn_s":
                    _, b, i = u
                    h, k = i // 2, i % 2
                    act.wait_ge(s_free, made(*u))
                    nc.scalar.activation(SQT[:, k, h * HALF:(h + 1) * HALF], SNT[:, k, h * HALF:(h + 1) * HALF],
                                         ACT.Square).then_inc(s_sqt, 1)
                elif kind == "dist":
                    _, b, h = u
                    act.wait_ge(s_free, made(*u))
                    nc.scalar.activation(DN[0:S, h * HALF:(h + 1) * HALF], DSQ[0:S, h * HALF:(h + 1) * HALF],
                                         ACT.Sqrt).then_inc(s_dn, 1)
                elif kind == "hidden":
                    _, b, h, m = u
                    n = h * HT + m
                    if m == 0 and b:
                        act.wait_ge(s_ready, made("out", b - 1, 2 * h + 1))
                    act.wait_ge(s_hid, b * 2 * HT + n + 1)
                    nc.scalar.activation(HGE[:, h, m], psS[:, (n % 4) // 2, n % 2], ACT.Gelu,
                                         bias=BEFF[:, m:m + 1]).then_inc(s_gelu, 1)

        @block.vector
        def _(dve):
            n_vec = [0]

            def vec(ins):
                ins.then_inc(s_vec, 1)
                n_vec[0] += 1

            def settled():
                dve.wait_ge(s_vec, n_vec[0])

            nc.vector.memset(V1[:, :, :, HD:32], 1.0).then_inc(s_ones, 1)
            dve.wait_ge(s_ctx_in, 16)
            sqc = ONT.rearrange("p g t -> p (g t)")[0:S, 0:B * D].rearrange("p (b d) -> p b d", b=B)
            vec(nc.vector.tensor_tensor(out=sqc, in0=CTX[:], in1=CTX[:], op=ALU.mult))
            settled()
            vec(nc.vector.tensor_reduce(AA[:], sqc, axis=AX.X, op=ALU.add))
            dve.wait_ge(s_bias_in, 48)
            vec(nc.vector.tensor_tensor(out=BIAS[:], in0=BIAS[:], in1=BIAS2[:], op=ALU.add))

            def mask(b, n):
                dve.wait_ge(s_sq, 2 * (b * NS + n) + 2)
                blk = A[:, (b * NS + n) % 2, :, 0:P]
                nc.vector.tensor_tensor(out=blk, in0=blk, in1=MASK[:].unsqueeze(1).to_broadcast([P, GH, P]),
                                        op=ALU.mult).then_inc(s_mask, 1)

            def heads_out(b, n):
                g, qc, kt = steps[n]
                o = b * NO + last_of.index(n)
                dve.wait_ge(s_av, b * NS + n + 1)
                nc.vector.transpose(TR.rearrange("p t e -> p (t e)"), psO[:, o % 2]).then_inc(s_o_read, 1)
                dve.wait_ge(s_o_read, o + 1)
                vec(nc.vector.tensor_scalar(ZT[:], TR[:, :, HD], Z_EPS, None, ALU.add))
                settled()
                vec(nc.vector.reciprocal(ZT[:], ZT[:]))
                settled()
                vec(nc.vector.tensor_tensor(out=TB[:, qc, :, HD * (g % 2):HD * (g % 2 + 1)], in0=TR[:, :, 0:HD],
                                            in1=ZT[:].unsqueeze(2).to_broadcast([P, HALF // 32, HD]), op=ALU.mult))
                settled()
                if g % 2:
                    nc.vector.transpose(ONT[:, g // 2, qc * HALF:(qc + 1) * HALF],
                                        TB[:, qc].rearrange("p t e -> p (t e)")).then_inc(s_ont, 1)

            def forward():
                for t in range(T):
                    dve.wait_ge(s_row, t + 1)
                    above, row = RSK[:, t], RSK[:, t + 1]
                    nc.vector.tensor_tensor(out=MIN2[:], in0=above[:, 1:CB + 1], in1=above[:, 0:CB], op=ALU.min).then_inc(s_pre, 1)
                    nc.vector.stream_shuffle(row[:, 0:1], above[:, CB:CB + 1], FROM_LEFT).then_inc(s_pre, 1)
                    dve.wait_ge(s_pre, 2 * t + 2)
                    nc.vector.tensor_tensor_scan(row[:, 1:CB + 1], MIN2[:], DSK[:, t], row[:, 0:1],
                                                 ALU.min, ALU.add).then_inc(s_row, 1)
                dve.wait_ge(s_row, T + 1)

            def moves():
                up, dg = RSK[:, 0:T, 1:CB + 1], RSK[:, 0:T, 0:CB]
                vec(nc.vector.tensor_tensor(out=M2, in0=up, in1=dg, op=ALU.min))
                vec(nc.vector.tensor_tensor(out=UPM, in0=up, in1=dg, op=ALU.is_lt))
                vec(nc.vector.memset(CODE[:, T], 1.0))
                vec(nc.vector.memset(CODE[:, 0:T, CB], 0.0))
                vec(nc.vector.memset(LEFT[:, :, CB], 0.0))
                settled()
                vec(nc.vector.tensor_scalar(UPM, UPM, -2.0, 1.0, ALU.mult, ALU.add))
                vec(nc.vector.tensor_tensor(out=LEFT[:, :, 0:CB], in0=M2, in1=RSK[:, 1:T + 1, 0:CB], op=ALU.is_gt))
                settled()
                vec(nc.vector.scalar_tensor_tensor(out=CODE[:, 0:T, 0:CB], in0=LEFT[:, :, 0:CB], scalar=0.0, in1=UPM,
                                                   op0=ALU.is_equal, op1=ALU.mult))
                vec(nc.vector.memset(PATH[:, T], 0.0))
                settled()
                nc.vector.tensor_copy(PATH[:, T, CB:CB + 1], START[:]).then_inc(s_mark, 1)
                vec(nc.vector.stream_shuffle(LEFT[:, 0:T - 1, CB], LEFT[:, 1:T, 0], FROM_RIGHT))
                vec(nc.vector.stream_shuffle(CODE[:, 0:T - 1, CB], CODE[:, 1:T, 0], FROM_RIGHT))
                settled()

            def backward():
                for s in range(T):
                    t = T - 1 - s
                    below, row = PATH[:, t + 1], PATH[:, t]
                    dve.wait_ge(s_mark, s + 1)
                    nc.vector.tensor_tensor(out=MOVE[:], in0=below, in1=CODE[:, t + 1], op=ALU.mult).then_inc(s_move, 1)
                    nc.vector.stream_shuffle(row[:, CB:CB + 1], below[:, 0:1], FROM_RIGHT).then_inc(s_enter, 1)
                    dve.wait_ge(s_move, s + 1)
                    nc.vector.scalar_tensor_tensor(out=ENTER[:], in0=MOVE[:, 0:CB], scalar=-1.0, in1=MOVE[:, 1:CB + 1],
                                                   op0=ALU.is_equal, op1=ALU.max).then_inc(s_enter, 1)
                    dve.wait_ge(s_enter, 2 * s + 2)
                    nc.vector.tensor_tensor_scan(row[:, 0:CB][:, ::-1], LEFT_BACK[:, s, 0:CB], ENTER[:, ::-1],
                                                 row[:, CB:CB + 1], ALU.mult, ALU.add).then_inc(s_mark, 1)

            for u in plan:
                kind = u[0]
                if kind in ITEM_KINDS and kind != "qk":
                    dve.wait_ge(s_ready, made(*u))
                    got = psW[:, bank(*u)]
                if kind == "context":
                    nc.vector.tensor_scalar(CTXT[:, u[1]], got[:, 0:KD * S].rearrange("p (k s) -> p k s", k=KD), -2.0, None,
                                            ALU.mult).then_inc(s_free, 1)
                elif kind == "w_exp":
                    nc.vector.tensor_copy(MIXA[:, 2 * u[1]:2 * u[1] + 2, 0:D], got.rearrange("p (r d) -> p r d", r=2)
                                          ).then_inc(s_free, 1)
                elif kind == "stats":
                    _, what, b, i = u
                    if what == "x" and i == 0:
                        dve.wait_ge(s_x_in, 16 * (b + 1))
                    if what == "student" and i == 0:
                        dve.wait_ge(s_free, made("wo", b, TT // 2 - 1))
                    if what == "ffn" and i == 0:
                        dve.wait_ge(s_free, made("along", b, TT // 2 - 1))
                    for t in (2 * i, 2 * i + 1):
                        ins = nc.vector.bn_stats(STATS[:, t], X[:, b, t])
                    vec(ins)
                elif kind == "variance":
                    settled()
                    for t in range(TT):
                        ins = nc.vector.bn_aggr(MV[:, t], STATS[:, t])
                    vec(ins)
                    settled()
                    nc.vector.tensor_scalar(VE[:], MV[:, :, 1], LN_EPS, None, ALU.add).then_inc(s_var, 1)
                elif kind == "rstd":
                    dve.wait_ge(s_sd, norm_of[u[1:]] + 1)
                    vec(nc.vector.reciprocal(RS[:], SD[:]))
                    settled()
                elif kind == "normal":
                    _, what, b, i = u
                    for t in (2 * i, 2 * i + 1):
                        ins = nc.vector.tensor_scalar(XN[:, t], X[:, b, t], MV[:, t, 0:1], RS[:, t:t + 1],
                                                      ALU.subtract, ALU.mult)
                    ins.then_inc(s_xn, 1)
                elif kind in ("turn_x", "turn_s", "turn_f"):
                    _, b, i = u
                    h, k = i // 2, i % 2
                    if kind == "turn_s" and i == 0 and b + 1 < B:
                        dve.wait_ge(s_parts_out, 64 * (b + 2))
                    dst = {"turn_x": XNT, "turn_s": SNT, "turn_f": XFT[b % 2]}[kind]
                    nc.vector.tensor_copy(dst[:, k, h * HALF:(h + 1) * HALF], got).then_inc(s_free, 1)
                elif kind == "qk":
                    _, b, i = u
                    m, s, h = i // 4, (i // 2) % 2, i % 2
                    if i == 0 and b >= 2:
                        dve.wait_ge(s_dist_out, 16 * (b - 1))
                    part = [QP[:, m, s, c, h * HALF:(h + 1) * HALF] for c in range(PARTS)]
                    dve.wait_ge(s_part1, b * 8 + i + 1)
                    if b or i:
                        dve.wait_ge(s_split, b * 8 + i)
                    nc.vector.scalar_tensor_tensor(out=R1, in0=psW[:, bank(*u)], scalar=0.25 if s == 0 else 1.0,
                                                   in1=part[0], op0=ALU.mult, op1=ALU.subtract).then_inc(s_free, 1)
                    dve.wait_ge(s_free, made(*u))
                    vec(nc.vector.tensor_copy(part[1], R1))
                    settled()
                    nc.vector.tensor_tensor(out=part[2], in0=R1, in1=part[1], op=ALU.subtract).then_inc(s_split, 1)
                elif kind == "value":
                    _, b, i = u
                    for j in range(2):
                        ins = nc.vector.tensor_copy(V1[:, 2 * i + j, :, 0:HD],
                                                    got[:, j * D:(j + 1) * D].rearrange("p (h e) -> p h e", h=NH))
                    ins.then_inc(s_free, 1)
                elif kind == "scores":
                    if u[2] in diag:
                        mask(*u[1:])
                elif kind == "products":
                    if u[2] in last_of:
                        heads_out(*u[1:])
                elif kind in ("wo", "along"):
                    _, b, i = u
                    xs = X[:, b, 2 * i:2 * i + 2]
                    nc.vector.tensor_tensor(out=xs, in0=xs, in1=got.rearrange("p (t d) -> p t d", t=2),
                                            op=ALU.add).then_inc(s_free, 1)
                elif kind == "dist":
                    _, b, h = u
                    nc.vector.tensor_scalar(DSQ[0:S, h * HALF:(h + 1) * HALF], got[0:S], AA[:, b:b + 1], 0.0,
                                            ALU.add, ALU.max).then_inc(s_free, 1)
                    if u == ("dist", B - 1, 1):
                        dve.wait_ge(s_dist_out, 16 * B)
                        nc.vector.memset(DSK, 0.0).then_inc(s_dsk0, 1)
                        vec(nc.vector.memset(RSK[:, 0], BIG))
                        settled()
                        nc.vector.tensor_copy(RSK[:, 0, 0:1], CORNER[:]).then_inc(s_row, 1)
                elif kind == "w1":
                    h, k = u[1] // 2, u[1] % 2
                    nc.vector.tensor_copy(W1E[:, k, h * HALF:(h + 1) * HALF], got).then_inc(s_free, 1)
                elif kind == "warp":
                    vec(nc.vector.tensor_tensor(out=BEFF[:], in0=UPB[:], in1=W1R[:, :, D], op=ALU.add))
                    dve.wait_ge(s_dsk_in, 16 * W_BLK)
                    forward()
                    moves()
                    backward()
                elif kind == "out":
                    _, b, i = u
                    if i == 0:
                        if b:
                            dve.wait_ge(s_free, made("out", b - 1, TT // 2 - 1))
                        vec(nc.vector.tensor_tensor(out=XB, in0=X[:, b], in1=BIAS[:].unsqueeze(1).to_broadcast([P, TT, D]),
                                                    op=ALU.add))
                        settled()
                    if b or i >= 2:
                        dve.wait_ge(s_out[i % 2], 16 * (b * TT // 4 + i // 2))
                    nc.vector.tensor_tensor(out=OUTB[:, i % 2], in0=XB[:, 2 * i:2 * i + 2],
                                            in1=got.rearrange("p (t d) -> p t d", t=2), op=ALU.add).then_inc(s_free, 1)

        @block.tensor
        def _(pe):
            pe.wait_ge(s_const, N_CONST)
            pe.wait_ge(s_ctx_in, 16)
            pe.wait_ge(s_ones, 1)
            we = WE.rearrange("p u j q -> p (u j q)")[:, 0:KD * HID].rearrange("p (k c r) -> p k r c", k=KD, r=8)

            def scores(b, n):
                g, qc, kt = steps[n]
                q0, N = span(n)
                G = b * NS + n
                if n % (NS // NG) == 0:
                    pe.wait_ge(s_stack[g % 2], 16 * 2 * len(Q_PART) * (2 * b + g // 2 + 1))
                for a in range(2):
                    if G:
                        pe.wait_ge(s_sq, 2 * G + a - 1)
                    for j in range(2):
                        ins = nc.tensor.matmul(psS[:, a, j, 0:N], KST[0:STACK, g % 2, 2 * a + j, kt * P:(kt + 1) * P],
                                               QST[0:STACK, g % 2, 2 * a + j, q0:q0 + N], start=True, stop=True)
                    ins.then_inc(s_qk, 1)

            def products(b, n):
                g, qc, kt = steps[n]
                q0, N = span(n)
                G = b * NS + n
                o = b * NO + 2 * g + qc
                if n == 0:
                    pe.wait_ge(s_free, made("value", b, TT // 2 - 1))
                pe.wait_ge(s_sq, 2 * G + 2)
                if n in diag:
                    pe.wait_ge(s_mask, b * len(diag) + diag.index(n) + 1)
                if kt == 0 and o >= 2:
                    pe.wait_ge(s_o_read, o - 1)
                for j in range(GH):
                    ins = nc.tensor.matmul(psO[32 * j:32 * j + 32, o % 2, q0 - qc * HALF:q0 - qc * HALF + N],
                                           V1[:, kt, GH * g + j], A[:, G % 2, j, 0:N],
                                           start=kt == 0, stop=n in last_of)
                ins.then_inc(s_av, 1)

            for u in plan:
                kind = u[0]
                if kind in ITEM_KINDS:
                    if item_of[u] >= 2:
                        pe.wait_ge(s_free, item_of[u] - 1)
                    W = psW[:, bank(*u)]
                if kind == "context":
                    for k in range(KD):
                        ins = nc.tensor.transpose(W[:, k * S:(k + 1) * S], CTX[:, u[1], k * P:(k + 1) * P], IDENT[0:S, 0:S])
                elif kind == "w_exp":
                    if u[1] == 0:
                        pe.wait_ge(s_we_in, 16)
                    for r in range(2):
                        for k in range(KD):
                            o = r * D + k * P
                            ins = nc.tensor.transpose(W[:, o:o + P], we[:, k, 2 * u[1] + r], IDENT[:])
                elif kind in ("turn_x", "turn_s", "turn_f"):
                    _, b, i = u
                    h, k = i // 2, i % 2
                    what = {"turn_x": "x", "turn_s": "student", "turn_f": "ffn"}[kind]
                    pe.wait_ge(s_xn, 4 * norm_of[what, b] + 2 * h + 2)
                    for t in range(4):
                        ins = nc.tensor.transpose(W[:, t * P:(t + 1) * P], XN[:, 4 * h + t, k * P:(k + 1) * P], IDENT[:])
                elif kind == "qk":
                    _, b, i = u
                    m, s, h = i // 4, (i // 2) % 2, i % 2
                    if i == 0:
                        pe.wait_ge(s_free, made("turn_x", b, 3))
                        if b == 0:
                            pe.wait_ge(s_w_in, 16 * (3 + 2 * GH))
                    for k in range(KD):
                        ins = nc.tensor.matmul(W, WQKV[:, k, s * D + m * P:s * D + (m + 1) * P],
                                               XNT[:, k, h * HALF:(h + 1) * HALF], start=k == 0, stop=k == KD - 1)
                elif kind == "value":
                    _, b, i = u
                    for j in range(2):
                        t = 2 * i + j
                        for k in range(KD):
                            ins = nc.tensor.matmul(W[:, j * D:(j + 1) * D], XNT[:, k, t * P:(t + 1) * P],
                                                   WQKV[:, k, 2 * D:3 * D], start=k == 0, stop=k == KD - 1)
                elif kind == "scores":
                    scores(*u[1:])
                elif kind == "products":
                    products(*u[1:])
                elif kind == "wo":
                    _, b, i = u
                    pe.wait_ge(s_ont, 4 * b + 3 + i // 2)
                    for j in range(2):
                        t = 2 * i + j
                        for g in range(2):
                            ins = nc.tensor.matmul(W[:, j * D:(j + 1) * D], ONT[:, g, t * P:(t + 1) * P], WOP[:, g],
                                                   start=g == 0, stop=g == 1)
                elif kind == "dist":
                    _, b, h = u
                    cols = slice(h * HALF, (h + 1) * HALF)
                    pe.wait_ge(s_free, made("turn_s", b, 2 * h + 1))
                    for k in range(KD):
                        nc.tensor.matmul(W[0:S], CTXT[:, b, k], SNT[:, k, cols], start=k == 0, stop=False)
                    pe.wait_ge(s_sqt, b * 4 + 2 * h + 2)
                    for k in range(KD):
                        ins = nc.tensor.matmul(W[0:S], ONES[:], SQT[:, k, cols], start=False, stop=k == KD - 1)
                elif kind == "w1":
                    h, k = u[1] // 2, u[1] % 2
                    if u[1] == 0:
                        pe.wait_ge(s_mix, N_MIX)
                        pe.wait_ge(s_mix_dma, N_MIX_DMA)
                    for r in range(4):
                        ins = nc.tensor.transpose(W[:, r * P:(r + 1) * P], W1R[:, 4 * h + r, k * P:(k + 1) * P], IDENT[:])
                elif kind == "along":
                    _, b, i = u
                    if b == 0 and i == 0:
                        pe.wait_ge(s_pt_in, 16)
                    for j in range(2):
                        t = 2 * i + j
                        ins = nc.tensor.matmul(W[:, j * D:(j + 1) * D], PT[:, b, t * P:(t + 1) * P], CTX[:, b],
                                               start=True, stop=True)
                elif kind == "hidden":
                    _, b, h, m = u
                    n = h * HT + m
                    if m == 0:
                        pe.wait_ge(s_free, made("turn_f", b, 2 * h + 1))
                    if b or n >= 4:
                        pe.wait_ge(s_gelu, b * 2 * HT + n - 3)
                    for k in range(KD):
                        ins = nc.tensor.matmul(psS[:, (n % 4) // 2, n % 2], W1E[:, k, m * P:(m + 1) * P],
                                               XFT[b % 2][:, k, h * HALF:(h + 1) * HALF], start=k == 0, stop=k == KD - 1)
                    ins.then_inc(s_hid, 1)
                elif kind == "out":
                    _, b, i = u
                    h = i // 2
                    pe.wait_ge(s_gelu, b * 2 * HT + (h + 1) * HT)
                    for j in range(2):
                        c = (2 * (i % 2) + j) * P
                        for m in range(HT):
                            ins = nc.tensor.matmul(W[:, j * D:(j + 1) * D], HGE[:, h, m, c:c + P], W2E[:, m, 0:D],
                                                   start=m == 0, stop=m == HT - 1)
                if kind in ITEM_KINDS:
                    ins.then_inc(s_ready, 1)


N_CONST = 5 + 2 + 2 * B
ARENA_WORDS = 27300
N_MIX = 1 + 2 * N_STAGE * 6
N_MIX_DMA = 16 * (2 * (3 * 1 + 3 * 16 + 3 * 2 + 1) + 1 + 2 * ((1 + 16) + (16 + 2) + (2 + 1)) + 1 + 2)
FROM_LEFT = [W_BLK] + list(range(W_BLK - 1)) + list(range(W_BLK, 32))
FROM_RIGHT = list(range(1, 32)) + [31]

_INS = ['x', 'ctx_1024', 'L0_attn_Wq', 'L0_attn_Wk', 'L0_attn_Wv', 'L0_attn_Wo', 'L0_ffn_W_exp', 'L0_ffn_b_exp',
        'L0_ffn_up_weights', 'L0_ffn_up_bias', 'L0_ffn_down_weights', 'L0_ffn_W_con', 'L0_ffn_b_con', 'L0_ffn_down_bias']


def kernel(**inputs):
    import numpy as np
    import concourse.bacc as bacc
    from concourse.bass_utils import run_bass_kernel_spmd

    nc = bacc.Bacc("TRN2", target_bir_lowering=False, num_devices=1)
    arrays, args = {}, []
    for name in _INS:
        a = np.ascontiguousarray(inputs[name])
        arrays[f"in_{name}"] = a
        args.append(nc.dram_tensor(f"in_{name}", a.shape, mybir.dt.from_np(a.dtype), kind="ExternalInput").ap())
    args.append(nc.dram_tensor("out_0", (B, L, D), F32, kind="ExternalOutput").ap())
    layer(nc, *args)
    r = run_bass_kernel_spmd(nc, [arrays], core_ids=[0])
    return r.results[0]["out_0"]
```

```python
from contextlib import ExitStack

import concourse.bass as bass
from concourse import mybir

F32 = mybir.dt.float32
BF16 = mybir.dt.bfloat16
ALU = mybir.AluOpType
ACT = mybir.ActivationFunctionType
AX = mybir.AxisListType

P = 128
B, L, D = 4, 1024, 256
NH, HD = 16, 16
S = 77
HID = 1024
KD = D // P
TT = L // P
HALF = 512
HT = HID // P
NG = 4
GH = NH // NG
PARTS = 3
Q_PART = [0, 0, 0, 1, 1, 2]
K_PART = [0, 1, 2, 0, 1, 0]
STACK = len(Q_PART) * HD
LN_EPS, Z_EPS = 1e-5, 1e-5
W_BLK = 16
CB = L // W_BLK
T = S + W_BLK - 1
BIG = 1e30
N_STAGE = 10
DC = D + 1
CH, GRP, RING = 23, 4, 8
A_PAIRS = 5
CP = CB + 2


def attention_steps():
    return [(g, qc, kt) for g in range(NG) for qc in range(L // HALF) for kt in range((qc + 1) * HALF // P)]


def norm_units(kind, b, before=()):
    stats = [("stats", kind, b, i) for i in range(TT // 2)]
    if before:
        stats = list(before[:2]) + sum(([s, u] for s, u in zip(stats, before[2:])), []) + stats[len(before) - 2:]
    return stats + [("variance", kind, b), ("rstd", kind, b)] + [("normal", kind, b, i) for i in range(TT // 2)]


def spread(parts, fill):
    plan = []
    for n, units in enumerate(parts):
        plan += units + fill[n * len(fill) // len(parts):(n + 1) * len(fill) // len(parts)]
    return plan


def make_plan():
    ns = len(attention_steps())
    front = lambda b: norm_units("x", b) + [("turn_x", b, i) for i in range(4)] + [("qk", b, i) for i in range(8)]

    def back(b, before=()):
        halves = [[("turn_s", b, 2 * h), ("turn_s", b, 2 * h + 1), ("dist", b, h)] for h in range(2)]
        return norm_units("student", b, before) + sum(halves, [])
    values = lambda b: [("value", b, i) for i in range(TT // 2)]
    both = lambda b: [("scores", b, 0, a) for a in range(2)]
    warp = [("warp_start",)] + [("forward", t) for t in range(T)] + [("moves",)] + [("backward", t) for t in reversed(range(T))]
    ready = lambda b: (norm_units("ffn", b, [("along", b, i) for i in range(TT // 2)])
                       + [("turn_f", b, i) for i in range(4)])
    plan = front(0) + [("w_exp", i) for i in range(4)] + values(0) + both(0)
    for b in range(B):
        steps = [([("scores", b, n + 1, 0)] if n + 1 < ns else []) + ([("products", b, n - 1)] if n else [])
                 + ([("scores", b, n + 1, 1)] if n + 1 < ns else []) for n in range(ns)] + [[("products", b, ns - 1)]]
        last = b + 1 == B
        fill = back(b - 1) if b else [("context", i) for i in range(B)]
        fill += [("w1", i) for i in range(4)] + [("bias",)] if last else front(b + 1)
        plan += steps[0] + spread(steps[1:-3], fill) + sum(steps[-3:], [])
        if not last:
            plan += values(b + 1) + both(b + 1)
        wo = [("wo", b, i) for i in range(TT // 2)]
        plan += back(b, wo) if last else wo
    plan += warp + ready(0)
    for b in range(B):
        plan += [("hidden", b, 0, m) for m in range(HT)]
        plan += spread([[("hidden", b, 1, m)] for m in range(HT)], ready(b + 1) if b + 1 < B else [])
        plan += [("out", b, i) for i in range(TT // 2)]
    return plan


ITEM_KINDS = ("context", "w_exp", "turn_x", "qk", "value", "wo", "turn_s", "dist", "w1", "along", "turn_f", "out")


def layer(nc, x, ctx_in, Wq, Wk, Wv, Wo, W_exp, b_exp, up_w, up_b, down_w, W_con, b_con, down_b, out):
    steps = attention_steps()
    NS = len(steps)
    diag = [n for n, (g, qc, kt) in enumerate(steps) if kt * P >= qc * HALF]
    last_of = [n for n, (g, qc, kt) in enumerate(steps) if (kt + 1) * P == (qc + 1) * HALF]
    NO = len(last_of)

    def span(n):
        g, qc, kt = steps[n]
        q0 = max(qc * HALF, kt * P)
        return q0, (qc + 1) * HALF - q0

    plan = make_plan()
    item_of = {u: k for k, u in enumerate(u for u in plan if u[0] in ITEM_KINDS)}
    norm_of = {u[1:3]: k for k, u in enumerate(u for u in plan if u[0] == "variance")}

    def made(*unit):
        return item_of[unit] + 1

    def bank(*unit):
        return item_of[unit] % 2

    qk_dram = nc.dram_tensor("qk_parts", (B, 2, PARTS, D, L), BF16, kind="Internal").ap()
    dist_dram = nc.dram_tensor("dist", (B, W_BLK * (T + 1) * CB), F32, kind="Internal").ap()
    path_dram = nc.dram_tensor("path", (B, W_BLK * (T + 1) * CB), BF16, kind="Internal").ap()

    def by_step(dram, b):
        return dram[b, 0:W_BLK * T * CB].rearrange("(w t c) -> w t c", w=W_BLK, t=T)

    def by_row(dram, b):
        return dram[b].rearrange("(w t c) -> t w c", w=W_BLK, t=T + 1)[0:S]

    mix_dram = nc.dram_tensor("mix", (HID, DC), F32, kind="Internal").ap()

    with ExitStack() as ctx:
        def sb(name, shape, dt=F32):
            return ctx.enter_context(nc.sbuf_tensor(name, shape, dt))

        def sem(name):
            return ctx.enter_context(nc.semaphore(name))

        X = sb("X", [P, B, TT, D])
        CTX = sb("CTX", [S, B, D])
        CTXT = sb("CTXT", [P, B, KD, S])
        AA = sb("AA", [S, B])
        IDENT = sb("IDENT", [P, P])
        ONES = sb("ONES", [P, S])
        MASK = sb("MASK", [P, P])
        WQKV = sb("WQKV", [P, KD, 3 * D])
        WOP = sb("WOP", [P, 2, D])
        BIAS = sb("BIAS", [P, D])
        UPB = sb("UPB", [P, HT])
        BEFF = sb("BEFF", [P, HT])
        BEXP = sb("BEXP", [P, 8])
        ZT = sb("ZT", [P, HALF // 32])
        MIXA = sb("MIXA", [P, 8, DC])
        MIXT = sb("MIXT", [P, 4, DC])
        W1R = sb("W1R", [P, 8, DC])
        W2E = sb("W2E", [P, HT, DC])
        COEF = sb("COEF", [P, 2 * N_STAGE, 4, 4])
        STATS = sb("STATS", [P, TT, 6])
        MV = sb("MV", [P, TT, 2])
        VE = sb("VE", [P, TT])
        SD = sb("SD", [P, TT])
        RS = sb("RS", [P, TT])
        CORNER = sb("CORNER", [P, 1])
        START = sb("START", [P, 1])
        MOVE = sb("MOVE", [P, CB + 1], BF16)
        ENTER = sb("ENTER", [P, CB], BF16)
        FIRST = sb("FIRST", [P, CP], BF16)
        XX = sb("XX", [P, TT * D + KD * L])
        XN = XX[:, 0:TT * D].rearrange("p (t d) -> p t d", t=TT)
        XNT = XX[:, TT * D:TT * D + KD * L].rearrange("p (k t) -> p k t", k=KD)

        ARENA = sb("ARENA", [P, ARENA_WORDS])
        at = [0]

        def view(words, dt=F32):
            a = ARENA[:, at[0]:at[0] + words]
            at[0] += words
            assert at[0] <= ARENA_WORDS, at[0]
            return a if dt == F32 else a.bitcast(dt)

        def view_back():
            return (view(KD * L).rearrange("p (k t) -> p k t", k=KD), view(KD * L).rearrange("p (k t) -> p k t", k=KD),
                    view(L), view(L))

        QP = view(2 * 2 * PARTS * L // 2, BF16).rearrange("p (m s c t) -> p m s c t", m=2, s=2, c=PARTS)
        at[0] = 0
        BACK = [view_back()] * (B - 1)
        R1 = view(HALF)
        operands = at[0]
        at[0] = 0
        DSK = view(2 * CH * CB).rearrange("p (u t c) -> p u t c", u=2, t=CH)
        CODE = view((T + 1) * CP // 2, BF16).rearrange("p (t c) -> p t c", t=T + 1)
        LEFT = XX[:, 0:T * CP // 2].bitcast(BF16).rearrange("p (t c) -> p t c", t=T)
        at[0] = operands
        QST = view(2 * GH * L // 2, BF16).rearrange("p (u j t) -> p u j t", u=2, j=GH)
        KST = view(2 * GH * L // 2, BF16).rearrange("p (u j t) -> p u j t", u=2, j=GH)
        V1 = view(TT * NH * 32).rearrange("p (t h e) -> p t h e", t=TT, h=NH)
        A = view(A_PAIRS * 2 * HALF).rearrange("p (u j q) -> p u j q", u=A_PAIRS, j=2)
        ONT = view(2 * L).rearrange("p (g t) -> p g t", g=2)
        TR = view(HALF).rearrange("p (t e) -> p t e", e=32)
        BIAS2 = TR.rearrange("p t e -> p (t e)")[:, 0:D]
        TB = view(2 * HALF).rearrange("p (q t e) -> p q t e", q=2, e=32)
        ZERO = TB.rearrange("p q t e -> p (q t e)")[:, 0:W_BLK * (T + 1) * CB // P]
        WE = A
        at[0] = operands
        BACK = BACK + [view_back()]
        XN_LAST = view(TT * D).rearrange("p (t d) -> p t d", t=TT)
        ROWS = view((RING + 1) * (CB + 1)).rearrange("p (t c) -> p t c", t=RING + 1)
        MINS = view(RING * CB).rearrange("p (t c) -> p t c", t=RING)
        NOT_UP = view(2 * GRP * CB // 2, BF16).rearrange("p (u t c) -> p u t c", u=2, t=GRP)
        at[0] = operands
        HGE = view(2 * HT * HALF).rearrange("p (u m t) -> p u m t", u=2, m=HT)
        OUTB = view(2 * 2 * D).rearrange("p (u t d) -> p u t d", u=2, t=2)
        XFT = [XNT, view(KD * L).rearrange("p (k t) -> p k t", k=KD)]
        XB = view(TT * D).rearrange("p (t d) -> p t d", t=TT)
        PT = view(B * L)[0:S].rearrange("p (b t) -> p b t", b=B)
        W1E = MIXA.rearrange("p r d -> p (r d)")[:, 0:KD * HID].rearrange("p (k h) -> p k h", k=KD)

        psS = ctx.enter_context(nc.psum_tensor("psS", [P, 2, 2, HALF], F32))
        psO = ctx.enter_context(nc.psum_tensor("psO", [P, 2, HALF], F32))
        psW = ctx.enter_context(nc.psum_tensor("psW", [P, 2, HALF], F32))

        s_const = sem("s_const")
        s_w_in = sem("s_w_in")
        s_ones = sem("s_ones")
        s_ctx_in = sem("s_ctx_in")
        s_we_in = sem("s_we_in")
        s_bias_in = sem("s_bias_in")
        s_x_in = [sem(f"s_x_in{b}") for b in range(B)]
        s_ready = sem("s_ready")
        s_free = sem("s_free")
        s_vec = sem("s_vec")
        s_var = sem("s_var")
        s_sd = sem("s_sd")
        s_xn = sem("s_xn")
        s_part1 = sem("s_part1")
        s_split = sem("s_split")
        s_parts_out = sem("s_parts_out")
        s_stack = [sem("s_stack_even"), sem("s_stack_odd")]
        s_qk = sem("s_qk")
        s_sq = sem("s_sq")
        s_mask = sem("s_mask")
        s_av = sem("s_av")
        s_o_read = sem("s_o_read")
        s_ont = sem("s_ont")
        s_sqt = sem("s_sqt")
        s_dn = sem("s_dn")
        s_dist_out = [sem(f"s_dist_out{b}") for b in range(B)]
        s_zero = sem("s_zero")
        s_dsk0 = sem("s_dsk0")
        s_ring = sem("s_ring")
        s_kind = sem("s_kind")
        s_twice = sem("s_twice")
        s_moves = sem("s_moves")
        s_dsk_in = [sem("s_dsk_even"), sem("s_dsk_odd")]
        s_pre = sem("s_pre")
        s_row = sem("s_row")
        s_move = sem("s_move")
        s_enter = sem("s_enter")
        s_mark = sem("s_mark")
        s_path_out = [sem(f"s_path_out{b}") for b in range(B)]
        s_pt_in = [sem(f"s_pt_in{b}") for b in range(B)]
        s_coef = [sem("s_coef_up"), sem("s_coef_down")]
        s_mix = sem("s_mix")
        s_mix_dma = sem("s_mix_dma")
        s_hid = sem("s_hid")
        s_gelu = sem("s_gelu")
        s_out = [sem("s_out_even"), sem("s_out_odd")]

        LAYOUT = {"A": (P, 1), "C": (16, 8), "D": (2, 64), "B": (1, P)}
        UP = [("A", [0, 1, 2]), ("C", [3, 4, 5]), ("D", [6, 7, 8]), ("B", [9])]
        DOWN = [(name, list(reversed(stages))) for name, stages in reversed(UP)]
        LOWBIT = {"A": 0, "C": 3, "D": 6, "B": 7}

        def pieces(name, dram, n):
            hi, lo = LAYOUT[name]
            if lo == 1:
                return [(0, P, dram.rearrange("(p r) c -> p r c", r=n))]
            if name == "C":
                v = dram.rearrange("(h r l) c -> l h r c", h=hi, r=n)
                return [(l * hi, hi, v[l]) for l in range(lo)]
            v = dram.rearrange("(h r l) c -> h l r c", h=hi, r=n)
            return [(h * lo, lo, v[h]) for h in range(hi)]

        block = ctx.enter_context(nc.Block())

        @block.sync
        def _(sp):
            sp.dma_start(X[:, 0], x[0].rearrange("(t p) d -> p t d", p=P)).then_inc(s_x_in[0], 16)
            for i, w in enumerate((Wq, Wk, Wv)):
                sp.dma_start(WQKV[:, :, i * D:(i + 1) * D], w.rearrange("(k p) n -> p k n", p=P)).then_inc(s_w_in, 16)
            sp.dma_start(CTX[:], ctx_in.rearrange("b s d -> s b d")).then_inc(s_ctx_in, 16)
            sp.dma_start(WE.rearrange("p u j q -> p (u j q)")[:, 0:KD * HID].rearrange("p (k h) -> p k h", k=KD),
                         W_exp.rearrange("(k p) h -> p k h", p=P)).then_inc(s_we_in, 16)
            for j in range(GH):
                for e in range(2):
                    sp.dma_start(WOP[32 * j + HD * e:32 * j + HD * (e + 1)],
                                 Wo.rearrange("(g e j d) n -> j e d g n", g=2, e=2, j=GH)[j, e]).then_inc(s_w_in, 16)
            sp.dma_start(BIAS[:], b_con.rearrange("(a n) -> a n", a=1).to_broadcast([P, D])).then_inc(s_bias_in, 16)
            sp.dma_start(BIAS2, down_b.rearrange("(a n) -> a n", a=1).to_broadcast([P, D])).then_inc(s_bias_in, 16)
            sp.dma_start(UPB[:], up_b.rearrange("(m p) -> p m", p=P), allow_slow_non_contiguous=True).then_inc(s_bias_in, 16)

            def parts_out(b, m):
                for i in range(2):
                    sp.wait_ge(s_split, b * 8 + 4 * m + 2 * i + 2)
                    dst = qk_dram[b, i].rearrange("c (m p) t -> m p c t", m=2)[m]
                    sp.dma_start(dst, QP[:, m, i]).then_inc(s_parts_out, 16)
                sp.wait_ge(s_parts_out, b * 64 + 32 * (m + 1))

            def stack_in(b, g):
                if b * NG + g >= 2:
                    sp.wait_ge(s_qk, (b * NG + g - 1) * 2 * NS // NG)
                for slot in range(len(Q_PART)):
                    rows = slice(slot * HD, (slot + 1) * HD)
                    for i, (dst, part) in enumerate(((QST, Q_PART), (KST, K_PART))):
                        src = qk_dram[b, i, part[slot]].rearrange("(g j d) t -> g d j t", g=NG, j=GH)[g]
                        sp.dma_start(dst[rows, g % 2], src).then_inc(s_stack[g % 2], 16)

            def dist_out(b):
                sp.wait_ge(s_dn, b * 2 + 2)
                if b == 0:
                    sp.wait_ge(s_zero, 16 * B)
                sp.dma_start(by_row(dist_dram, b), BACK[b][3][0:S].rearrange("p (w c) -> p w c", w=W_BLK)).then_inc(s_dist_out[b], 16)

            def coefficients(u):
                for name, stages in (UP, DOWN)[u]:
                    for st in stages:
                        for p0, n, src in pieces(name, (up_w, down_w)[u][st].rearrange("q o i -> q (o i)"), 4):
                            sp.dma_start(COEF[p0:p0 + n, u * N_STAGE + st], src).then_inc(s_coef[u], 16)

            coefficients(0)
            sp.wait_ge(s_const, N_CONST)
            for b in range(B):
                sp.dma_start(dist_dram[b].rearrange("(p n) -> p n", p=P), ZERO).then_inc(s_zero, 16)
            parts_out(0, 0)
            stack_in(0, 0)
            stack_in(0, 1)
            parts_out(0, 1)
            coefficients(1)
            for b in range(B):
                stack_in(b, 2)
                if 0 < b < B - 1:
                    dist_out(b - 1)
                stack_in(b, 3)
                if b == B - 1:
                    dist_out(b - 1)
                if b + 1 < B:
                    for m in range(2):
                        parts_out(b + 1, m)
                        stack_in(b + 1, m)
            dist_out(B - 1)

            for t0, t1 in ((T // 2, T), (0, T // 2)):
                sp.wait_ge(s_mark, T - t0 + 1)
                for b in range(B):
                    sp.dma_start(by_step(path_dram, b)[:, t0:t1], CODE[32 * b:32 * b + W_BLK, t0 + 1:t1 + 1, 1:CB + 1]).then_inc(s_path_out[b], 16)
            for b in range(B):
                for i in range(TT // 2):
                    sp.wait_ge(s_free, made("out", b, i))
                    sp.dma_start(out[b].rearrange("(t p) d -> p t d", p=P)[:, 2 * i:2 * i + 2], OUTB[:, i % 2]).then_inc(s_out[i % 2], 16)
            for i in range(2):
                sp.wait_ge(s_out[i], 16 * B * TT // 4)

        @block.gpsimd
        def _(pool):
            n_const = [0]

            def const(ins):
                ins.then_inc(s_const, 1)
                n_const[0] += 1

            const(pool.memset(IDENT[:], 0.0))
            const(pool.memset(MASK[:], 1.0))
            const(pool.memset(ONES[:], 1.0))
            const(pool.memset(START[:], 0.0))
            const(pool.memset(ZERO, 0.0))
            const(pool.memset(CORNER[:], BIG))
            pool.wait_ge(s_const, n_const[0])
            const(pool.affine_select(out=IDENT[:], in_=IDENT[:], compare_op=ALU.not_equal, fill=1.0, base=0,
                                     pattern=[[-1, P]], channel_multiplier=1))
            const(pool.affine_select(out=MASK[:], in_=MASK[:], compare_op=ALU.is_ge, fill=0.0, base=0,
                                     pattern=[[1, P]], channel_multiplier=-1))
            for b in range(B):
                for col, at_w, v in ((START, W_BLK - 1, 1.0), (CORNER, 0, 0.0)):
                    pool.wait_ge(s_const, n_const[0])
                    const(pool.affine_select(out=col[:], in_=col[:], compare_op=ALU.not_equal, fill=v,
                                             base=-32 * b - at_w, pattern=[[0, 1]], channel_multiplier=1))
            assert n_const[0] == N_CONST

            for b in range(1, B):
                pool.wait_ge(s_x_in[b - 1], 16)
                pool.dma_start(X[:, b], x[b].rearrange("(t p) d -> p t d", p=P)).then_inc(s_x_in[b], 16)

            n_mix, n_dma = [0], [0]

            def load(dst, src):
                pool.dma_start(dst, src).then_inc(s_mix_dma, 16)
                n_dma[0] += 16

            def loaded():
                pool.wait_ge(s_mix_dma, n_dma[0])

            def mixed():
                pool.wait_ge(s_mix, n_mix[0])

            def mix(ins):
                ins.then_inc(s_mix, 1)
                n_mix[0] += 1

            load(BEXP[:], b_exp.rearrange("(p r) -> p r", r=8))

            def butterfly(plan, which, dst, width):
                for k, (name, stages) in enumerate(plan):
                    if k:
                        mixed()
                        for p0, n, v in pieces(plan[k - 1][0], mix_dram[:, 0:width], 8):
                            load(v, dst[p0:p0 + n, :, 0:width])
                        loaded()
                        for p0, n, v in pieces(name, mix_dram[:, 0:width], 8):
                            load(MIXA[p0:p0 + n, :, 0:width], v)
                    loaded()
                    src, to = MIXA, dst
                    if len(stages) % 2 == 0:
                        raise AssertionError("a group has an odd number of stages")
                    for st in stages:
                        c_n = 1 << (st - LOWBIT[name])
                        def halves(t):
                            return t[:, :, 0:width].rearrange("p (a x c) d -> p x a c d", x=2, c=c_n)
                        cf = COEF[:, which * N_STAGE + st].rearrange("p (a c) k -> p k a c", c=c_n)
                        tmp = MIXT[:, :, 0:width].rearrange("p (a c) d -> p a c d", c=c_n)
                        old, new = halves(src), halves(to)
                        shape = [P, 4 // c_n, c_n, width]
                        for o in range(2):
                            own = cf[:, 3 * o].unsqueeze(3).to_broadcast(shape)
                            other = cf[:, (1 + o) if which == 0 else (2 - o)].unsqueeze(3).to_broadcast(shape)
                            mixed()
                            mix(pool.tensor_tensor(out=new[:, o], in0=old[:, o], in1=own, op=ALU.mult))
                            mix(pool.tensor_tensor(out=tmp, in0=old[:, 1 - o], in1=other, op=ALU.mult))
                            mixed()
                            mix(pool.tensor_tensor(out=new[:, o], in0=new[:, o], in1=tmp, op=ALU.add))
                        src, to = to, src

            pool.wait_ge(s_free, made("w_exp", 3))
            loaded()
            mix(pool.tensor_copy(MIXA[:, :, D], BEXP[:]))
            pool.wait_ge(s_coef[0], 16 * N_COEF)
            butterfly(UP, 0, W1R, DC)
            mixed()
            load(MIXA[:, :, 0:D], W_con.rearrange("(r p) d -> p r d", p=P))
            pool.wait_ge(s_coef[1], 16 * N_COEF)
            butterfly(DOWN, 1, W2E, D)
            mixed()
            for p0, n, v in pieces("A", mix_dram[:, 0:D], 8):
                load(v, W2E[p0:p0 + n, :, 0:D])
            loaded()
            for p0, n, v in pieces("B", mix_dram[:, 0:D], 8):
                load(W2E[p0:p0 + n, :, 0:D], v)
            loaded()
            assert (n_mix[0], n_dma[0]) == (N_MIX, N_MIX_DMA), (n_mix, n_dma)

            def distances(k, b):
                pool.dma_start(DSK[32 * b:32 * b + W_BLK, k % 2],
                               by_step(dist_dram, b)[:, k * CH:(k + 1) * CH]).then_inc(s_dsk_in[k % 2], 16)

            for b in range(B - 1):
                pool.wait_ge(s_dist_out[b], 16)
            pool.memset(DSK, 0.0).then_inc(s_dsk0, 1)
            pool.wait_ge(s_dsk0, 1)
            for k in range(2):
                for b in range(B - 1):
                    distances(k, b)
            pool.wait_ge(s_dist_out[B - 1], 16)
            for k in range(2):
                distances(k, B - 1)
            for g in range(T // GRP):
                rows = slice(g * GRP, (g + 1) * GRP)
                pool.wait_ge(s_kind, 2 * (g + 1))
                pool.tensor_tensor(out=CODE[:, rows, 0:CB], in0=NOT_UP[:, g % 2], in1=NOT_UP[:, g % 2], op=ALU.add).then_inc(s_twice, 1)
                pool.wait_ge(s_twice, g + 1)
                pool.tensor_tensor(out=CODE[:, rows, 0:CB], in0=CODE[:, rows, 0:CB], in1=LEFT[:, rows, 0:CB],
                                   op=ALU.subtract).then_inc(s_moves, 1)
                for k in range(2, T // CH):
                    if g == (k - 1) * CH // GRP:
                        pool.wait_ge(s_row, (k - 1) * CH + 1)
                        for b in range(B):
                            distances(k, b)
            for b in range(B):
                pool.wait_ge(s_path_out[b], 2 * 16)
                pool.dma_start(PT[:, b].rearrange("p (w c) -> p w c", w=W_BLK), by_row(path_dram, b)).then_inc(s_pt_in[b], 16)

        @block.scalar
        def _(act):
            for u in plan:
                kind = u[0]
                if kind == "variance":
                    act.wait_ge(s_var, norm_of[u[1:]] + 1)
                    nc.scalar.activation(SD[:], VE[:], ACT.Sqrt).then_inc(s_sd, 1)
                elif kind == "qk":
                    _, b, i = u
                    m, s, h = i // 4, (i // 2) % 2, i % 2
                    if i == 0 and b >= 2:
                        act.wait_ge(s_dist_out[b - 2], 16)
                    act.wait_ge(s_ready, made(*u))
                    nc.scalar.activation(QP[:, m, s, 0, h * HALF:(h + 1) * HALF], psW[:, bank(*u)], ACT.Copy,
                                         scale=0.25 if s == 0 else 1.0).then_inc(s_part1, 1)
                elif kind == "scores":
                    _, b, n, a = u
                    q0, N = span(n)
                    G = b * NS + n
                    act.wait_ge(s_qk, 2 * G + a + 1)
                    if 2 * G + a >= A_PAIRS:
                        act.wait_ge(s_av, (2 * G + a - A_PAIRS) // 2 + 1)
                    nc.scalar.activation(A[:, (2 * G + a) % A_PAIRS, :, 0:N], psS[:, a, :, 0:N], ACT.Square).then_inc(s_sq, 1)
                elif kind == "turn_s":
                    _, b, i = u
                    h, k = i // 2, i % 2
                    act.wait_ge(s_free, made(*u))
                    SNT, SQT = BACK[b][0:2]
                    nc.scalar.activation(SQT[:, k, h * HALF:(h + 1) * HALF], SNT[:, k, h * HALF:(h + 1) * HALF],
                                         ACT.Square).then_inc(s_sqt, 1)
                elif kind == "dist":
                    _, b, h = u
                    act.wait_ge(s_free, made(*u))
                    DSQ, DN = BACK[b][2:4]
                    nc.scalar.activation(DN[0:S, h * HALF:(h + 1) * HALF], DSQ[0:S, h * HALF:(h + 1) * HALF],
                                         ACT.Sqrt).then_inc(s_dn, 1)
                elif kind == "hidden":
                    _, b, h, m = u
                    n = h * HT + m
                    if m == 0 and b == 0:
                        act.wait_ge(s_dist_out[B - 1], 16)
                    if m == 0 and b:
                        act.wait_ge(s_ready, made("out", b - 1, 2 * h + 1))
                    act.wait_ge(s_hid, b * 2 * HT + n + 1)
                    nc.scalar.activation(HGE[:, h, m], psS[:, (n % 4) // 2, n % 2], ACT.Gelu,
                                         bias=BEFF[:, m:m + 1]).then_inc(s_gelu, 1)

        @block.vector
        def _(dve):
            n_vec = [0]

            def vec(ins):
                ins.then_inc(s_vec, 1)
                n_vec[0] += 1

            def settled():
                dve.wait_ge(s_vec, n_vec[0])

            nc.vector.memset(V1[:, :, :, HD:32], 1.0).then_inc(s_ones, 1)

            def context_norms():
                dve.wait_ge(s_ctx_in, 16)
                sqc = ONT.rearrange("p g t -> p (g t)")[0:S, 0:B * D].rearrange("p (b d) -> p b d", b=B)
                vec(nc.vector.tensor_tensor(out=sqc, in0=CTX[:], in1=CTX[:], op=ALU.mult))
                settled()
                vec(nc.vector.tensor_reduce(AA[:], sqc, axis=AX.X, op=ALU.add))

            def mask(b, n, a):
                pair = 2 * (b * NS + n) + a
                dve.wait_ge(s_sq, pair + 1)
                blk = A[:, pair % A_PAIRS, :, 0:P]
                nc.vector.tensor_tensor(out=blk, in0=blk, in1=MASK[:].unsqueeze(1).to_broadcast([P, 2, P]),
                                        op=ALU.mult).then_inc(s_mask, 1)

            def heads_out(b, n):
                g, qc, kt = steps[n]
                o = b * NO + last_of.index(n)
                if (b, n) == (0, last_of[0]):
                    dve.wait_ge(s_zero, 16 * B)
                dve.wait_ge(s_av, b * NS + n + 1)
                nc.vector.transpose(TR.rearrange("p t e -> p (t e)"), psO[:, o % 2]).then_inc(s_o_read, 1)
                dve.wait_ge(s_o_read, o + 1)
                vec(nc.vector.tensor_scalar(ZT[:], TR[:, :, HD], Z_EPS, None, ALU.add))
                settled()
                vec(nc.vector.reciprocal(ZT[:], ZT[:]))
                settled()
                vec(nc.vector.tensor_tensor(out=TB[:, qc, :, HD * (g % 2):HD * (g % 2 + 1)], in0=TR[:, :, 0:HD],
                                            in1=ZT[:].unsqueeze(2).to_broadcast([P, HALF // 32, HD]), op=ALU.mult))
                settled()
                if g % 2:
                    nc.vector.transpose(ONT[:, g // 2, qc * HALF:(qc + 1) * HALF],
                                        TB[:, qc].rearrange("p t e -> p (t e)")).then_inc(s_ont, 1)

            def warp_start():
                vec(nc.vector.memset(ROWS[:, 0], BIG))
                vec(nc.vector.memset(FIRST[:], 0.0))
                settled()
                vec(nc.vector.tensor_copy(FIRST[:, CB + 1:CP], START[:]))
                nc.vector.tensor_copy(ROWS[:, 0, 0:1], CORNER[:]).then_inc(s_row, 1)

            def find_moves(g, part):
                r, rows = g * GRP % RING, slice(g * GRP, (g + 1) * GRP)
                if part == 0:
                    if g and r == 0:
                        nc.vector.tensor_copy(ROWS[:, 0], ROWS[:, RING]).then_inc(s_ring, 1)
                        dve.wait_ge(s_ring, g * GRP // RING)
                    if g >= 2:
                        dve.wait_ge(s_moves, g - 1)
                    nc.vector.tensor_tensor(out=NOT_UP[:, g % 2], in0=ROWS[:, r:r + GRP, 1:CB + 1], in1=ROWS[:, r:r + GRP, 0:CB],
                                            op=ALU.is_ge).then_inc(s_kind, 1)
                elif part == 1:
                    nc.vector.tensor_tensor(out=LEFT[:, rows, 0:CB], in0=MINS[:, r:r + GRP],
                                            in1=ROWS[:, r + 1:r + GRP + 1, 0:CB], op=ALU.is_gt).then_inc(s_kind, 1)

            def forward(t):
                above = ROWS[:, (t - 1) % RING + 1 if t else 0]
                row, least = ROWS[:, t % RING + 1], MINS[:, t % RING]
                if t % CH == 0:
                    k = t // CH
                    dve.wait_ge(s_dsk_in[k % 2], 16 * B * (k // 2 + 1))
                dve.wait_ge(s_row, t + 1)
                nc.vector.tensor_tensor(out=least, in0=above[:, 1:CB + 1], in1=above[:, 0:CB], op=ALU.min).then_inc(s_pre, 1)
                nc.vector.stream_shuffle(row[:, 0:1], above[:, CB:CB + 1], FROM_LEFT).then_inc(s_pre, 1)
                dve.wait_ge(s_pre, 2 * t + 2)
                nc.vector.tensor_tensor_scan(row[:, 1:CB + 1], least, DSK[:, t // CH % 2, t % CH], row[:, 0:1],
                                             ALU.min, ALU.add).then_inc(s_row, 1)
                if t >= GRP:
                    find_moves(t // GRP - 1, t % GRP)

            def moves():
                dve.wait_ge(s_row, T + 1)
                for part in range(2):
                    find_moves(T // GRP - 1, part)
                dve.wait_ge(s_moves, T // GRP)
                vec(nc.vector.memset(CODE[:, T], 2.0))
                vec(nc.vector.memset(CODE[:, T - 1, CB:CB + 1], 0.0))
                vec(nc.vector.memset(LEFT[:, T - 1, CB:CB + 1], 0.0))
                vec(nc.vector.stream_shuffle(LEFT[:, 0:T - 1, CB], LEFT[:, 1:T, 0], FROM_RIGHT))
                vec(nc.vector.stream_shuffle(CODE[:, 0:T - 1, CB], CODE[:, 1:T, 0], FROM_RIGHT))
                settled()
                nc.vector.tensor_copy(ENTER[:, 0:1], START[:]).then_inc(s_mark, 1)

            def backward(t):
                n = T - 1 - t
                below, row = CODE[:, t + 2] if t + 1 < T else FIRST[:], CODE[:, t + 1]
                dve.wait_ge(s_mark, n + 1)
                nc.vector.scalar_tensor_tensor(out=MOVE[:], in0=row[:, 0:CB + 1], scalar=-1.0, in1=below[:, 1:CP],
                                               op0=ALU.add, op1=ALU.mult).then_inc(s_move, 1)
                nc.vector.stream_shuffle(row[:, CB + 1:CP], below[:, 1:2], FROM_RIGHT).then_inc(s_enter, 1)
                dve.wait_ge(s_move, n + 1)
                nc.vector.scalar_tensor_tensor(out=ENTER[:], in0=MOVE[:, 0:CB], scalar=-1.0, in1=MOVE[:, 1:CB + 1],
                                               op0=ALU.is_equal, op1=ALU.max).then_inc(s_enter, 1)
                dve.wait_ge(s_enter, 2 * n + 2)
                nc.vector.tensor_tensor_scan(row[:, 1:CB + 1][:, ::-1], LEFT[:, t, 1:CB + 1][:, ::-1], ENTER[:, ::-1],
                                             row[:, CB + 1:CP], ALU.mult, ALU.add).then_inc(s_mark, 1)

            for u in plan:
                kind = u[0]
                if kind in ITEM_KINDS and kind != "qk":
                    dve.wait_ge(s_ready, made(*u))
                    got = psW[:, bank(*u)]
                if kind == "context":
                    if u[1] == 0:
                        context_norms()
                    nc.vector.tensor_scalar(CTXT[:, u[1]], got[:, 0:KD * S].rearrange("p (k s) -> p k s", k=KD), -2.0, None,
                                            ALU.mult).then_inc(s_free, 1)
                elif kind == "w_exp":
                    if u[1] == 0:
                        dve.wait_ge(s_bias_in, 48)
                        vec(nc.vector.tensor_tensor(out=BIAS[:], in0=BIAS[:], in1=BIAS2, op=ALU.add))
                    nc.vector.tensor_copy(MIXA[:, 2 * u[1]:2 * u[1] + 2, 0:D], got.rearrange("p (r d) -> p r d", r=2)
                                          ).then_inc(s_free, 1)
                elif kind == "stats":
                    _, what, b, i = u
                    if what == "x" and i == 0:
                        dve.wait_ge(s_x_in[b], 16)
                    if what == "student":
                        dve.wait_ge(s_free, made("wo", b, i))
                    if what == "ffn":
                        dve.wait_ge(s_free, made("along", b, i))
                    for t in (2 * i, 2 * i + 1):
                        ins = nc.vector.bn_stats(STATS[:, t], X[:, b, t])
                    vec(ins)
                elif kind == "variance":
                    settled()
                    for t in range(TT):
                        ins = nc.vector.bn_aggr(MV[:, t], STATS[:, t])
                    vec(ins)
                    settled()
                    nc.vector.tensor_scalar(VE[:], MV[:, :, 1], LN_EPS, None, ALU.add).then_inc(s_var, 1)
                elif kind == "rstd":
                    dve.wait_ge(s_sd, norm_of[u[1:]] + 1)
                    vec(nc.vector.reciprocal(RS[:], SD[:]))
                    settled()
                elif kind == "normal":
                    _, what, b, i = u
                    for t in (2 * i, 2 * i + 1):
                        dst = XN_LAST if (what, b) == ("student", B - 1) else XN
                        ins = nc.vector.tensor_scalar(dst[:, t], X[:, b, t], MV[:, t, 0:1], RS[:, t:t + 1],
                                                      ALU.subtract, ALU.mult)
                    ins.then_inc(s_xn, 1)
                elif kind in ("turn_x", "turn_s", "turn_f"):
                    _, b, i = u
                    h, k = i // 2, i % 2
                    if kind == "turn_s" and i == 0 and b + 1 < B:
                        dve.wait_ge(s_parts_out, 64 * (b + 2))
                    dst = {"turn_x": XNT, "turn_s": BACK[b][0], "turn_f": XFT[b % 2]}[kind]
                    nc.vector.tensor_copy(dst[:, k, h * HALF:(h + 1) * HALF], got).then_inc(s_free, 1)
                elif kind == "qk":
                    _, b, i = u
                    m, s, h = i // 4, (i // 2) % 2, i % 2
                    if i == 0 and b >= 2:
                        dve.wait_ge(s_dist_out[b - 2], 16)
                    part = [QP[:, m, s, c, h * HALF:(h + 1) * HALF] for c in range(PARTS)]
                    dve.wait_ge(s_part1, b * 8 + i + 1)
                    if b or i:
                        dve.wait_ge(s_split, b * 8 + i)
                    nc.vector.scalar_tensor_tensor(out=R1, in0=psW[:, bank(*u)], scalar=0.25 if s == 0 else 1.0,
                                                   in1=part[0], op0=ALU.mult, op1=ALU.subtract).then_inc(s_free, 1)
                    dve.wait_ge(s_free, made(*u))
                    vec(nc.vector.tensor_copy(part[1], R1))
                    settled()
                    nc.vector.tensor_tensor(out=part[2], in0=R1, in1=part[1], op=ALU.subtract).then_inc(s_split, 1)
                elif kind == "value":
                    _, b, i = u
                    for j in range(2):
                        ins = nc.vector.tensor_copy(V1[:, 2 * i + j, :, 0:HD],
                                                    got[:, j * D:(j + 1) * D].rearrange("p (h e) -> p h e", h=NH))
                    ins.then_inc(s_free, 1)
                elif kind == "scores":
                    if u[2] in diag:
                        mask(*u[1:])
                elif kind == "products":
                    if u[2] in last_of:
                        heads_out(*u[1:])
                elif kind in ("wo", "along"):
                    _, b, i = u
                    xs = X[:, b, 2 * i:2 * i + 2]
                    nc.vector.tensor_tensor(out=xs, in0=xs, in1=got.rearrange("p (t d) -> p t d", t=2),
                                            op=ALU.add).then_inc(s_free, 1)
                elif kind == "dist":
                    _, b, h = u
                    DSQ = BACK[b][2]
                    nc.vector.tensor_scalar(DSQ[0:S, h * HALF:(h + 1) * HALF], got[0:S], AA[:, b:b + 1], 0.0,
                                            ALU.add, ALU.max).then_inc(s_free, 1)
                elif kind == "w1":
                    h, k = u[1] // 2, u[1] % 2
                    nc.vector.tensor_copy(W1E[:, k, h * HALF:(h + 1) * HALF], got).then_inc(s_free, 1)
                elif kind == "bias":
                    vec(nc.vector.tensor_tensor(out=BEFF[:], in0=UPB[:], in1=W1R[:, :, D], op=ALU.add))
                elif kind == "warp_start":
                    warp_start()
                elif kind == "forward":
                    forward(*u[1:])
                elif kind == "moves":
                    moves()
                elif kind == "backward":
                    backward(*u[1:])
                elif kind == "out":
                    _, b, i = u
                    if i == 0:
                        if b:
                            dve.wait_ge(s_free, made("out", b - 1, TT // 2 - 1))
                        vec(nc.vector.tensor_tensor(out=XB, in0=X[:, b], in1=BIAS[:].unsqueeze(1).to_broadcast([P, TT, D]),
                                                    op=ALU.add))
                        settled()
                    if b or i >= 2:
                        dve.wait_ge(s_out[i % 2], 16 * (b * TT // 4 + i // 2))
                    nc.vector.tensor_tensor(out=OUTB[:, i % 2], in0=XB[:, 2 * i:2 * i + 2],
                                            in1=got.rearrange("p (t d) -> p t d", t=2), op=ALU.add).then_inc(s_free, 1)

        @block.tensor
        def _(pe):
            pe.wait_ge(s_const, N_CONST)
            pe.wait_ge(s_ones, 1)
            we = WE.rearrange("p u j q -> p (u j q)")[:, 0:KD * HID].rearrange("p (k c r) -> p k r c", k=KD, r=8)

            def scores(b, n, a):
                g, qc, kt = steps[n]
                q0, N = span(n)
                G = b * NS + n
                if n % (NS // NG) == 0 and a == 0:
                    pe.wait_ge(s_stack[g % 2], 16 * 2 * len(Q_PART) * (2 * b + g // 2 + 1))
                if G:
                    pe.wait_ge(s_sq, 2 * G + a - 1)
                for j in range(2):
                    ins = nc.tensor.matmul(psS[:, a, j, 0:N], KST[0:STACK, g % 2, 2 * a + j, kt * P:(kt + 1) * P],
                                           QST[0:STACK, g % 2, 2 * a + j, q0:q0 + N], start=True, stop=True)
                ins.then_inc(s_qk, 1)

            def products(b, n):
                g, qc, kt = steps[n]
                q0, N = span(n)
                G = b * NS + n
                o = b * NO + 2 * g + qc
                if n == 0:
                    pe.wait_ge(s_free, made("value", b, TT // 2 - 1))
                pe.wait_ge(s_sq, 2 * G + 2)
                if n in diag:
                    pe.wait_ge(s_mask, 2 * (b * len(diag) + diag.index(n) + 1))
                if kt == 0 and o >= 2:
                    pe.wait_ge(s_o_read, o - 1)
                for j in range(GH):
                    ins = nc.tensor.matmul(psO[32 * j:32 * j + 32, o % 2, q0 - qc * HALF:q0 - qc * HALF + N],
                                           V1[:, kt, GH * g + j], A[:, (2 * G + j // 2) % A_PAIRS, j % 2, 0:N],
                                           start=kt == 0, stop=n in last_of)
                ins.then_inc(s_av, 1)

            for u in plan:
                kind = u[0]
                if kind in ITEM_KINDS:
                    if item_of[u] >= 2:
                        pe.wait_ge(s_free, item_of[u] - 1)
                    W = psW[:, bank(*u)]
                if kind == "context":
                    if u[1] == 0:
                        pe.wait_ge(s_ctx_in, 16)
                    for k in range(KD):
                        ins = nc.tensor.transpose(W[:, k * S:(k + 1) * S], CTX[:, u[1], k * P:(k + 1) * P], IDENT[0:S, 0:S])
                elif kind == "w_exp":
                    if u[1] == 0:
                        pe.wait_ge(s_we_in, 16)
                    for r in range(2):
                        for k in range(KD):
                            o = r * D + k * P
                            ins = nc.tensor.transpose(W[:, o:o + P], we[:, k, 2 * u[1] + r], IDENT[:])
                elif kind in ("turn_x", "turn_s", "turn_f"):
                    _, b, i = u
                    h, k = i // 2, i % 2
                    what = {"turn_x": "x", "turn_s": "student", "turn_f": "ffn"}[kind]
                    pe.wait_ge(s_xn, 4 * norm_of[what, b] + 2 * h + 2)
                    src = XN_LAST if (what, b) == ("student", B - 1) else XN
                    for t in range(4):
                        ins = nc.tensor.transpose(W[:, t * P:(t + 1) * P], src[:, 4 * h + t, k * P:(k + 1) * P], IDENT[:])
                elif kind == "qk":
                    _, b, i = u
                    m, s, h = i // 4, (i // 2) % 2, i % 2
                    if i == 0:
                        pe.wait_ge(s_free, made("turn_x", b, 3))
                        if b == 0:
                            pe.wait_ge(s_w_in, 16 * (3 + 2 * GH))
                    for k in range(KD):
                        ins = nc.tensor.matmul(W, WQKV[:, k, s * D + m * P:s * D + (m + 1) * P],
                                               XNT[:, k, h * HALF:(h + 1) * HALF], start=k == 0, stop=k == KD - 1)
                elif kind == "value":
                    _, b, i = u
                    for j in range(2):
                        t = 2 * i + j
                        for k in range(KD):
                            ins = nc.tensor.matmul(W[:, j * D:(j + 1) * D], XNT[:, k, t * P:(t + 1) * P],
                                                   WQKV[:, k, 2 * D:3 * D], start=k == 0, stop=k == KD - 1)
                elif kind == "scores":
                    scores(*u[1:])
                elif kind == "products":
                    products(*u[1:])
                elif kind == "wo":
                    _, b, i = u
                    pe.wait_ge(s_ont, 4 * b + 3 + i // 2)
                    for j in range(2):
                        t = 2 * i + j
                        for g in range(2):
                            ins = nc.tensor.matmul(W[:, j * D:(j + 1) * D], ONT[:, g, t * P:(t + 1) * P], WOP[:, g],
                                                   start=g == 0, stop=g == 1)
                elif kind == "dist":
                    _, b, h = u
                    cols = slice(h * HALF, (h + 1) * HALF)
                    pe.wait_ge(s_free, made("turn_s", b, 2 * h + 1))
                    SNT, SQT = BACK[b][0:2]
                    for k in range(KD):
                        nc.tensor.matmul(W[0:S], CTXT[:, b, k], SNT[:, k, cols], start=k == 0, stop=False)
                    pe.wait_ge(s_sqt, b * 4 + 2 * h + 2)
                    for k in range(KD):
                        ins = nc.tensor.matmul(W[0:S], ONES[:], SQT[:, k, cols], start=False, stop=k == KD - 1)
                elif kind == "w1":
                    h, k = u[1] // 2, u[1] % 2
                    if u[1] == 0:
                        pe.wait_ge(s_mix, N_MIX)
                        pe.wait_ge(s_mix_dma, N_MIX_DMA)
                    for r in range(4):
                        ins = nc.tensor.transpose(W[:, r * P:(r + 1) * P], W1R[:, 4 * h + r, k * P:(k + 1) * P], IDENT[:])
                elif kind == "along":
                    _, b, i = u
                    if i == 0:
                        pe.wait_ge(s_pt_in[b], 16)
                    for j in range(2):
                        t = 2 * i + j
                        ins = nc.tensor.matmul(W[:, j * D:(j + 1) * D], PT[:, b, t * P:(t + 1) * P], CTX[:, b],
                                               start=True, stop=True)
                elif kind == "hidden":
                    _, b, h, m = u
                    n = h * HT + m
                    if m == 0:
                        pe.wait_ge(s_free, made("turn_f", b, 2 * h + 1))
                    if b or n >= 4:
                        pe.wait_ge(s_gelu, b * 2 * HT + n - 3)
                    for k in range(KD):
                        ins = nc.tensor.matmul(psS[:, (n % 4) // 2, n % 2], W1E[:, k, m * P:(m + 1) * P],
                                               XFT[b % 2][:, k, h * HALF:(h + 1) * HALF], start=k == 0, stop=k == KD - 1)
                    ins.then_inc(s_hid, 1)
                elif kind == "out":
                    _, b, i = u
                    h = i // 2
                    pe.wait_ge(s_gelu, b * 2 * HT + (h + 1) * HT)
                    for j in range(2):
                        c = (2 * (i % 2) + j) * P
                        for m in range(HT):
                            ins = nc.tensor.matmul(W[:, j * D:(j + 1) * D], HGE[:, h, m, c:c + P], W2E[:, m, 0:D],
                                                   start=m == 0, stop=m == HT - 1)
                if kind in ITEM_KINDS:
                    ins.then_inc(s_ready, 1)


N_CONST = 6 + 2 + 2 * B
ARENA_WORDS = 27686
N_MIX = 1 + 2 * N_STAGE * 6
N_MIX_DMA = 16 * (1 + 2 * ((1 + 8) + (8 + 2) + (2 + 1)) + 1 + 2)
N_COEF = 3 * 1 + 3 * 8 + 3 * 2 + 1
FROM_LEFT = [W_BLK] + list(range(W_BLK - 1)) + list(range(W_BLK, 32))
FROM_RIGHT = list(range(1, 32)) + [31]

_INS = ['x', 'ctx_1024', 'L0_attn_Wq', 'L0_attn_Wk', 'L0_attn_Wv', 'L0_attn_Wo', 'L0_ffn_W_exp', 'L0_ffn_b_exp',
        'L0_ffn_up_weights', 'L0_ffn_up_bias', 'L0_ffn_down_weights', 'L0_ffn_W_con', 'L0_ffn_b_con', 'L0_ffn_down_bias']


def kernel(**inputs):
    import numpy as np
    import concourse.bacc as bacc
    from concourse.bass_utils import run_bass_kernel_spmd

    nc = bacc.Bacc("TRN2", target_bir_lowering=False, num_devices=1)
    arrays, args = {}, []
    for name in _INS:
        a = np.ascontiguousarray(inputs[name])
        arrays[f"in_{name}"] = a
        args.append(nc.dram_tensor(f"in_{name}", a.shape, mybir.dt.from_np(a.dtype), kind="ExternalInput").ap())
    args.append(nc.dram_tensor("out_0", (B, L, D), F32, kind="ExternalOutput").ap())
    layer(nc, *args)
    r = run_bass_kernel_spmd(nc, [arrays], core_ids=[0])
    return r.results[0]["out_0"]
```
